# Optimizing a Trainium2 kernel written in Bass

```python
import numpy as np
import jax
import jax.numpy as jnp

def _softmax(x, axis=-1):
    return jax.nn.softmax(x, axis=axis)

def _gelu(x):
    return jax.nn.gelu(x, approximate=True)

def _silu(x):
    return jax.nn.silu(x)

def _sigmoid(x):
    return jax.nn.sigmoid(x)

def _layernorm(x, axis=-1, eps=1e-05):
    m = jnp.mean(x, axis=axis, keepdims=True)
    v = jnp.var(x, axis=axis, keepdims=True)
    return (x - m) / jnp.sqrt(v + eps)

def _scatter_add(tgt, idx, src, axis=0):
    return tgt.at[idx].add(src)

def _segment_sum(src, seg, n):
    return jax.ops.segment_sum(src, seg, n)
kernel_name = 'mk_gnn_preln_d1_gnn_r8_5683ff'

def setup_inputs(seed: int=0):
    np.random.seed(seed)
    _w = jnp.asarray

    def _rec_inputs():
        import jax
        import jax.numpy as jnp
        _gk = jax.random.key(seed)
        x = -8.776e-05 + 1 * jax.random.normal(jax.random.fold_in(_gk, 1), (1250, 512), jnp.float32)
        src = jax.random.randint(jax.random.fold_in(_gk, 2), (40000,), 0, 1250, jnp.int32)
        dst = jnp.minimum((1250 * jax.random.uniform(jax.random.fold_in(_gk, 3), (40000,)) ** 2.0).astype(jnp.int32), 9999)
        _o = jnp.argsort(dst, stable=True)
        src = src[_o]
        dst = dst[_o]
        return (x, src, dst)
    x, src, dst = _rec_inputs()

    def _L0_gnn_setup():
        import jax, jax.numpy as jnp
        import numpy as np
        N_NODES = 1250
        N_EDGES = 20000
        D_FEAT = 512
        OUT_CH = 512
        key = jax.random.key(seed)
        k1, k2, k3, k4 = jax.random.split(key, 4)
        x = jax.random.normal(k1, (N_NODES, D_FEAT), dtype=jnp.float32)
        edge_index = jax.random.randint(k2, (N_EDGES, 2), 0, N_NODES, dtype=jnp.int64)
        W = jax.random.normal(k3, (OUT_CH, 2 * D_FEAT), dtype=jnp.float32) / np.sqrt(2 * D_FEAT)
        b = jax.random.normal(k4, (OUT_CH,), dtype=jnp.float32) * 0.01
        return {'x': x, 'edge_index': edge_index, 'num_local_nodes': N_NODES, 'W': W, 'b': b}
    _L0_gnn_all = _L0_gnn_setup()
    _L0_gnn_in = {k: v for k, v in _L0_gnn_all.items() if k in ('W', 'b')}
    del _L0_gnn_all
    return {'x': x, 'src': src, 'dst': dst, 'L0_gnn_W': _L0_gnn_in['W'], 'L0_gnn_b': _L0_gnn_in['b']}

def reference(x, src, dst, L0_gnn_W, L0_gnn_b):
    import jax
    import jax.numpy as jnp

    def _L0_gnn_ref(x, edge_index, num_local_nodes, W, b):
        import jax, jax.numpy as jnp
        import numpy as np
        N_NODES = 1250
        N_EDGES = 20000
        D_FEAT = 512
        OUT_CH = 512
        src = edge_index[:, 0]
        tgt = edge_index[:, 1]
        x_i = x[src]
        x_j = x[tgt]
        x_ij = jnp.concatenate([x_i, x_j], axis=1)
        m_ij = jax.nn.relu(x_ij @ W.T + b)
        out = jax.ops.segment_sum(m_ij, src, num_segments=num_local_nodes)
        return out
    edge_index_t = jnp.stack([src, dst], axis=1)
    h = jnp.maximum(_layernorm(x, axis=-1), 0.0)
    x = x + _L0_gnn_ref(h, edge_index_t, 1250, L0_gnn_W, L0_gnn_b)
    return x

_drawn_inputs = setup_inputs


def setup_inputs(seed=0):
    import zlib

    import numpy as np

    out = dict(_drawn_inputs(seed))
    spreads = {}
    factors = {'L0_gnn_b': 4.142}
    for name, (base, spread) in spreads.items():
        noise = np.random.default_rng([zlib.crc32(name.encode()), seed]).standard_normal(out[name].shape)
        drawn = base * np.exp(spread * noise) if base else spread * noise
        out[name] = jnp.asarray(drawn.astype(out[name].dtype))
    for name, factor in factors.items():
        out[name] = (out[name] * factor).astype(out[name].dtype)
    return out
```

```python
from contextlib import ExitStack

import concourse.bass as bass
from concourse import mybir

ALU = mybir.AluOpType
ACT = mybir.ActivationFunctionType
F32 = mybir.dt.float32
F16 = mybir.dt.float16
BF16 = mybir.dt.bfloat16
I32 = mybir.dt.int32

P = 128
EPS = 1e-5
GROUP = 2


def bass_gnn_edge_messages(nc, x, src, dst, wt, bias, out):
    N, D = x.shape
    (E,) = src.shape
    KC = D // P
    NB = -(-N // P)
    LAST = N - (NB - 1) * P
    EP = max(p for p in range(1, P + 1) if E % p == 0)
    EC = E // EP
    GS = GROUP * P
    NG = (E + NB * (GS - 1)) // GS
    NT = NG * GROUP
    assert NT <= 512 and EC % NB == 0 and D == 512

    PR = 8
    CPB = EC // NB
    R = 8
    R4 = 4
    TURNS = NT // R

    v_rows = nc.dram_tensor("v_rows", [N, D], F32, kind="Internal").ap()

    with ExitStack() as ctx:
        def sb(name, shape, dt):
            return ctx.enter_context(nc.sbuf_tensor(name, shape, dt))

        def sem(name):
            return ctx.enter_context(nc.semaphore(name))

        bank = [ctx.enter_context(nc.psum_tensor(f"bank{i}", [P, 512], F32)) for i in range(8)]

        acc = sb("acc", [P, NB, D], F32)
        w_sb = sb("w_sb", [P, 2 * KC, D], F32)
        b_sb = sb("b_sb", [P, D], F32)
        iota1 = sb("iota1", [P, P], F32)
        iota16 = sb("iota16", [P, NT], F16)
        pcol = sb("pcol", [P, 1], F32)
        ident = sb("ident", [P, P], F32)
        earlier = sb("earlier", [P, P], F32)
        ones = sb("ones", [P, 512], F32)
        group_no = sb("group_no", [1, NG], F32)
        eps_col = sb("eps_col", [P, 1], F32)

        src_i = sb("src_i", [EP, EC], I32)
        dst_i = sb("dst_i", [EP, EC], I32)
        tmp_i = sb("tmp_i", [EP, EC], I32)
        blk_i = sb("blk_i", [EP, EC], I32)
        blk_f = sb("blk_f", [EP, EC], F32)
        node1 = sb("node1", [EP, EC], F32)
        dst_f = sb("dst_f", [EP, EC], F32)
        in_blk = sb("in_blk", [EP, NB, EC], F32)
        cnt = sb("cnt", [EP, NB], F32)
        running = sb("running", [EP, NB, EC], F32)
        pos = sb("pos", [EP, EC], F32)
        pos_i = sb("pos_i", [EP, EC], I32)
        pos_hi_i = sb("pos_hi_i", [EP, EC], I32)
        pos_lo = sb("pos_lo", [EP, EC], F32)
        pos_hi = sb("pos_hi", [EP, EC], F32)
        tot_i = sb("tot_i", [P, NB], I32)
        ngr_i = sb("ngr_i", [P, NB], I32)
        ngr = sb("ngr", [P, NB], F32)
        g_end = sb("g_end", [P, NB], F32)
        g_start = sb("g_start", [P, NB], F32)
        off = sb("off", [P, NB], F32)
        gb_f = sb("gb_f", [1, NG], F32)
        gb_i = sb("gb_i", [1, NG], I32)

        stats = sb("stats", [P, NB, 6], F32)
        mv = sb("mv", [P, NB, 2], F32)
        std = sb("std", [P, NB], F32)
        rstd = sb("rstd", [P, NB], F32)
        nmr = sb("nmr", [P, NB], F32)
        h = sb("h", [P, 2, D], F32)
        hT = sb("hT", [P, 2, D], F32)
        v_out = sb("v_out", [P, 2, D], F32)
        u_f = sb("u_f", [P, 2, D], F32)
        u_r = sb("u_r", [P, 2, D], F32)
        u3 = sb("u3", [P, 3, NB, D], BF16)

        hot_lo_d = sb("hot_lo_d", [EP, PR, P], F16)
        hot_lo_s = sb("hot_lo_s", [EP, PR, P], F16)
        hot_hi = sb("hot_hi", [EP, PR, NT], F16)

        slot_dst = sb("slot_dst", [P, NT + R], I32)
        slot_node1 = sb("slot_node1", [P, NT], F32)
        window = sb("window", [P, R], I32)
        v_t = sb("v_t", [P, R, D], F32)
        hot = sb("hot", [P, R, P], F32)
        hotT = sb("hotT", [P, R4, P], BF16)
        pre = sb("pre", [P, R4, D], F32)
        msg = sb("msg", [P, R4, D], F32)

        place_d, place_s = bank[0], bank[1]
        ps_hT, ps_u, ps_v, ps_cnt = bank[2], bank[3], bank[4], bank[5]
        ps_exp = [bank[i] for i in (0, 1, 2, 3)]
        ps_hotT = [bank[i] for i in (4, 5)]
        ps_agg = [bank[i] for i in (6, 7)]

        src_in, dst_in, x_in, w_in, b_in = (sem(n) for n in ("src_in", "dst_in", "x_in", "w_in", "b_in"))
        rest_zero = sem("rest_zero")
        consts = sem("consts")
        masks = sem("masks")
        dve_step = sem("dve_step")
        counted = sem("counted")
        summed = sem("summed")
        mv_ready, std_ready, norm_ready = sem("mv_ready"), sem("std_ready"), sem("norm_ready")
        h_ready, hT_done, hT_ready = sem("h_ready"), sem("hT_done"), sem("hT_ready")
        u_done, v_done = sem("u_done"), sem("v_done")
        u_biased, u_hi, u_rest, u_mid, u_low = (sem(n) for n in ("u_biased", "u_hi", "u_rest", "u_mid", "u_low"))
        v_copied = sem("v_copied")
        v_stored = [sem(f"v_stored{i}") for i in range(2)]
        operands, placed = sem("operands"), sem("placed")
        tables, nodes_ready = sem("tables"), sem("nodes_ready")
        groups_ready = sem("groups_ready")
        window_ready = sem("window_ready")
        v_landed = [sem(f"v_landed{i}") for i in range(R)]
        hot_ready, hotT_done, hotT_ready = sem("hot_ready"), sem("hotT_done"), sem("hotT_ready")
        spread, pre_ready, msg_ready = sem("spread"), sem("pre_ready"), sem("msg_ready")
        slot_free = sem("slot_free")
        gathers_let = sem("gathers_let")
        summed_tiles, added = sem("summed_tiles"), sem("added")
        out_stored = sem("out_stored")

        def turns(eng, body, first, last_rest):
            for j in range(R):
                body(j, j, 0)
            with eng.Fori(1, TURNS) as i:
                for j in range(R):
                    body(i * R + j, j, i)
            for k in range(TURNS * R, last_rest):
                body(k, k % R, k // R)

        block = ctx.enter_context(nc.Block())

        @block.sync
        def _(sp):
            sp.dma_start(src_i[:], src.rearrange("(p c) -> p c", p=EP)).then_inc(src_in, 16)
            sp.dma_start(dst_i[:], dst.rearrange("(p c) -> p c", p=EP)).then_inc(dst_in, 16)
            sp.dma_start(acc[:, 0:NB - 1, :],
                         x[0:(NB - 1) * P, :].rearrange("(b p) d -> p b d", p=P)).then_inc(x_in, 16)
            sp.wait_ge(rest_zero, 1)
            sp.dma_start(acc[0:LAST, NB - 1, :], x[(NB - 1) * P:N, :]).then_inc(x_in, 16)
            sp.dma_start(w_sb[:], wt.rearrange("(c p) o -> p c o", p=P)).then_inc(w_in, 16)
            sp.dma_start(b_sb[:], bias.rearrange("(a d) -> a d", a=1).to_broadcast([P, D])).then_inc(b_in, 16)
            for g in range(NB):
                rows = P if g < NB - 1 else LAST
                sp.wait_ge(v_copied, g + 1)
                sp.dma_start(v_rows[g * P:g * P + rows, :], v_out[0:rows, g % 2, :]).then_inc(v_stored[g % 2], 16)
            sp.wait_ge(added, NG)
            sp.dma_start(out[0:(NB - 1) * P, :].rearrange("(b p) d -> p b d", p=P),
                         acc[:, 0:NB - 1, :]).then_inc(out_stored, 16)
            sp.dma_start(out[(NB - 1) * P:N, :], acc[0:LAST, NB - 1, :]).then_inc(out_stored, 16)
            sp.wait_ge(out_stored, 32)

        @block.gpsimd
        def _(pool):
            nc.gpsimd.memset(acc[:, NB - 1, :], 0.0).then_inc(rest_zero, 1)
            nc.gpsimd.iota(iota1[:], pattern=[[1, P]], base=1, channel_multiplier=0,
                           allow_small_or_imprecise_dtypes=True).then_inc(consts, 1)
            nc.gpsimd.iota(pcol[:], pattern=[[1, 1]], base=1, channel_multiplier=1,
                           allow_small_or_imprecise_dtypes=True).then_inc(consts, 1)
            nc.gpsimd.iota(iota16[:], pattern=[[1, NT]], base=0, channel_multiplier=0,
                           allow_small_or_imprecise_dtypes=True).then_inc(consts, 1)
            nc.gpsimd.iota(group_no[:], pattern=[[1, NG]], base=0, channel_multiplier=0,
                           allow_small_or_imprecise_dtypes=True).then_inc(consts, 1)
            for g in range(NB):
                pool.wait_ge(u_hi, g + 1)
                nc.gpsimd.tensor_tensor(u_r[:, g % 2, :], u_f[:, g % 2, :], u3[:, 0, g, :],
                                        ALU.subtract).then_inc(u_rest, 1)
                pool.wait_ge(u_mid, g + 1)
                nc.gpsimd.tensor_tensor(u3[:, 2, g, :], u_r[:, g % 2, :], u3[:, 1, g, :],
                                        ALU.subtract).then_inc(u_low, 1)
            pool.wait_ge(v_stored[0], 16 * -(-NB // 2))
            pool.wait_ge(v_stored[1], 16 * (NB // 2))
            pool.wait_ge(window_ready, 1)

            def gather(t, j, i):
                if not (isinstance(t, int) and t < R):
                    pool.wait_ge(slot_free, t - R + 1)
                    pool.sem_inc(gathers_let, 1)
                nc.gpsimd.indirect_dma_start(
                    out=v_t[:, j, :], out_offset=None, in_=v_rows,
                    in_offset=bass.IndirectOffsetOnAxis(ap=window[:, j:j + 1], axis=0),
                ).then_inc(v_landed[j], 16)

            turns(pool, gather, 0, NT)

        @block.vector
        def _(dve):
            chain = [0]

            def link(ins):
                chain[0] += 1
                ins.then_inc(dve_step, 1)
                dve.wait_ge(dve_step, chain[0])

            nc.vector.memset(ones[:], 1.0)
            nc.vector.memset(eps_col[:], EPS)
            nc.vector.memset(slot_dst[:, NT:NT + R], 0)
            dve.wait_ge(consts, 4)
            nc.vector.tensor_scalar(ident[:], iota1[:], pcol[:], None, ALU.is_equal)
            nc.vector.tensor_scalar(earlier[:], iota1[:], pcol[:], None, ALU.is_gt).then_inc(masks, 1)

            dve.wait_ge(src_in, 16)
            nc.vector.tensor_scalar(blk_i[:], src_i[:], 7, None, ALU.arith_shift_right)
            link(nc.vector.tensor_scalar(tmp_i[:], src_i[:], P - 1, None, ALU.bitwise_and))
            nc.vector.tensor_scalar(node1[:], tmp_i[:], 1.0, None, ALU.add)
            link(nc.vector.tensor_copy(blk_f[:], blk_i[:]))
            for b in range(NB):
                last = nc.vector.tensor_scalar(in_blk[:, b, :], blk_f[:], float(b), None, ALU.is_equal,
                                               ALU.add, accum_out=cnt[:, b:b + 1])
            last.then_inc(counted, 1)
            dve.wait_ge(dst_in, 16)
            nc.vector.tensor_copy(dst_f[:], dst_i[:])

            dve.wait_ge(x_in, 32)
            for b in range(NB):
                rows = P if b < NB - 1 else LAST
                last = nc.vector.bn_stats(stats[0:rows, b, :], acc[0:rows, b, :])
            link(last)
            nc.vector.memset(mv[:, NB - 1, :], 0.0)
            link(nc.vector.bn_aggr(mv[:, 0, :], stats[:, 0, :]))
            for b in range(1, NB):
                rows = P if b < NB - 1 else LAST
                last = nc.vector.bn_aggr(mv[0:rows, b, :], stats[0:rows, b, :])
            last.then_inc(mv_ready, 1)

            dve.wait_ge(counted, 1)
            dve.wait_ge(summed, 1)
            link(nc.vector.tensor_scalar(tot_i[:], ps_cnt[:, 16:16 + NB], float(GS - 1), None, ALU.add))
            link(nc.vector.tensor_scalar(ngr_i[:], tot_i[:], GS.bit_length() - 1, None, ALU.arith_shift_right))
            link(nc.vector.tensor_copy(ngr[:], ngr_i[:]))
            link(nc.vector.tensor_tensor_scan(g_end[:], ones[:, 0:NB], ngr[:], 0.0, ALU.mult, ALU.add))
            link(nc.vector.tensor_tensor(g_start[:], g_end[:], ngr[:], ALU.subtract))
            link(nc.vector.tensor_scalar(off[:], g_start[:], float(GS), -1.0, ALU.mult, ALU.add))
            link(nc.vector.tensor_tensor(off[0:EP, :], off[0:EP, :], ps_cnt[0:EP, 0:NB], ALU.add))
            for b in range(NB):
                last = nc.vector.tensor_tensor_scan(running[:, b, :], ones[0:EP, 0:EC], in_blk[:, b, :],
                                                    off[0:EP, b:b + 1], ALU.mult, ALU.add)
            link(last)
            link(nc.vector.tensor_tensor(running[:], running[:], in_blk[:], ALU.mult))
            link(nc.vector.tensor_reduce(pos[:], running[:].rearrange("p b c -> p c b"),
                                         mybir.AxisListType.X, ALU.add))
            link(nc.vector.tensor_copy(pos_i[:], pos[:]))
            nc.vector.tensor_scalar(pos_hi_i[:], pos_i[:], 7, None, ALU.arith_shift_right)
            link(nc.vector.tensor_scalar(tmp_i[:], pos_i[:], P - 1, None, ALU.bitwise_and))
            nc.vector.tensor_copy(pos_hi[:], pos_hi_i[:])
            link(nc.vector.tensor_copy(pos_lo[:], tmp_i[:]))

            link(nc.vector.tensor_scalar(gb_f[:], group_no[:], g_end[0:1, 0:1], None, ALU.is_ge))
            for b in range(1, NB - 1):
                link(nc.vector.scalar_tensor_tensor(gb_f[:], group_no[:], g_end[0:1, b:b + 1], gb_f[:],
                                                    ALU.is_ge, ALU.add))
            nc.vector.tensor_copy(gb_i[:], gb_f[:]).then_inc(groups_ready, 1)

            dve.wait_ge(std_ready, 1)
            link(nc.vector.reciprocal(rstd[:], std[:]))
            nc.vector.scalar_tensor_tensor(nmr[:], mv[:, :, 0], -1.0, rstd[:], ALU.mult,
                                           ALU.mult).then_inc(norm_ready, 1)

            def place(c, j, g):
                if not (isinstance(c, int) and c < PR):
                    dve.wait_ge(placed, c - PR + 1)
                cc = bass.ds(c, 1)
                nc.vector.tensor_scalar(hot_hi[:, j % PR, :], iota16[0:EP, :], pos_hi[:, cc], None, ALU.is_equal)
                nc.vector.tensor_scalar(hot_lo_d[:, j % PR, :], iota16[0:EP, 0:P], pos_lo[:, cc], dst_f[:, cc],
                                        ALU.is_equal, ALU.mult)
                nc.vector.tensor_scalar(hot_lo_s[:, j % PR, :], iota16[0:EP, 0:P], pos_lo[:, cc], node1[:, cc],
                                        ALU.is_equal, ALU.mult).then_inc(operands, 1)

            dve.wait_ge(b_in, 16)

            def prepare(g, par, first):
                for j in range(CPB):
                    place(g * CPB + j, j, g)
                    if j == CPB - 1:
                        dve.wait_ge(u_done, g + 1)
                        if not first:
                            dve.wait_ge(u_low, g - 1)
                        nc.vector.tensor_tensor(u_f[:, par, :], ps_u[:], b_sb[:], ALU.add).then_inc(u_biased, 1)

            prepare(0, 0, True)
            prepare(1, 1, True)
            with dve.Fori(1, NB // 2) as g2:
                prepare(g2 * 2, 0, False)
                prepare(g2 * 2 + 1, 1, False)

            dve.wait_ge(placed, EC)
            nc.vector.tensor_copy(slot_dst[:, 0:NT], place_d[:, 0:NT]).then_inc(tables, 1)
            nc.vector.tensor_copy(slot_node1[:], place_s[:, 0:NT]).then_inc(nodes_ready, 1)
            dve.wait_ge(nodes_ready, 1)

            def one_hot(t, j):
                if not (isinstance(t, int) and t < R):
                    dve.wait_ge(summed_tiles, t - R + 1)
                nc.vector.tensor_scalar(hot[:, j % R, :], iota1[:], slot_node1[:, bass.ds(t, 1)], None,
                                        ALU.is_equal).then_inc(hot_ready, 1)

            one_hot(0, 0)
            one_hot(1, 1)

            def step(k, j, i):
                static = isinstance(k, int)
                if not static or k + 2 < NT:
                    one_hot(k + 2, j + 2)
                if not static or k < NT:
                    dve.wait_ge(v_landed[j], 16 * (i + 1))
                    dve.wait_ge(spread, k + 1)
                    if not (static and k < R4):
                        dve.wait_ge(msg_ready, k - R4 + 1)
                    nc.vector.tensor_tensor(pre[:, j % R4, :], v_t[:, j, :], ps_exp[j % R4][:],
                                            ALU.add).then_inc(pre_ready, 1)
                if j % 2 == 0 and not (static and k < 4):
                    s = k // 2 - 2 if static else i * (R // 2) + (j // 2 - 2)
                    dve.wait_ge(summed_tiles, 2 * s + 2)
                    if not (static and s == 0):
                        dve.wait_ge(added, s)
                    b = dve.value_load(gb_i[0:1, bass.ds(s, 1)], min_val=0, max_val=NB - 1)
                    a = acc[:, bass.ds(b, 1), :].rearrange("p a d -> p (a d)")
                    nc.vector.tensor_tensor(a, a, ps_agg[(j // 2) % 2][:], ALU.add).then_inc(added, 1)

            turns(dve, step, 0, NT + 3)

        @block.scalar
        def _(act):
            act.wait_ge(mv_ready, 1)
            nc.scalar.activation(std[:], mv[:, :, 1], ACT.Sqrt, bias=eps_col[:]).then_inc(std_ready, 1)
            act.wait_ge(norm_ready, 1)

            def normalize(g, par):
                nc.scalar.activation(h[:, par, :], acc[:, bass.ds(g, 1), :].rearrange("p a d -> p (a d)"),
                                     ACT.Relu, bias=nmr[:, bass.ds(g, 1)],
                                     scale=rstd[:, bass.ds(g, 1)]).then_inc(h_ready, 1)

            for g in range(NB):
                par = g % 2
                if g >= 2:
                    act.wait_ge(hT_done, g - 1)
                normalize(g, par)
                act.wait_ge(hT_done, g + 1)
                if g >= 2:
                    act.wait_ge(v_done, g - 1)
                nc.scalar.copy(hT[:, par, :], ps_hT[:]).then_inc(hT_ready, 1)
                act.wait_ge(v_done, g + 1)
                if g >= 2:
                    act.wait_ge(v_stored[par], 16 * (g // 2))
                nc.scalar.copy(v_out[:, par, :], ps_v[:]).then_inc(v_copied, 1)
                act.wait_ge(u_biased, g + 1)
                nc.scalar.copy(u3[:, 0, g, :], u_f[:, par, :]).then_inc(u_hi, 1)
                act.wait_ge(u_rest, g + 1)
                nc.scalar.copy(u3[:, 1, g, :], u_r[:, par, :]).then_inc(u_mid, 1)

            act.wait_ge(tables, 1)
            nc.scalar.copy(window[:], slot_dst[:, 0:R]).then_inc(window_ready, 1)

            def turned(t, j):
                act.wait_ge(hotT_done, t + 1)
                if not (isinstance(t, int) and t < R4):
                    act.wait_ge(spread, t - R4 + 1)
                nc.scalar.copy(hotT[:, j % R4, :], ps_hotT[j % 2][:, 0:P]).then_inc(hotT_ready, 1)

            turned(0, 0)

            def step(k, j, i):
                static = isinstance(k, int)
                if not static or k + 1 < NT:
                    turned(k + 1, j + 1)
                act.wait_ge(pre_ready, k + 1)
                if not (static and k < R4):
                    act.wait_ge(summed_tiles, k - R4 + 1)
                nc.scalar.activation(msg[:, j % R4, :], pre[:, j % R4, :], ACT.Relu).then_inc(msg_ready, 1)
                nc.scalar.copy(window[:, j:j + 1], slot_dst[:, bass.ds(k + R, 1)]).then_inc(slot_free, 1)

            turns(act, step, 0, NT)

        @block.tensor
        def _(pe):
            pe.wait_ge(masks, 1)
            pe.wait_ge(counted, 1)
            nc.tensor.matmul(ps_cnt[0:EP, 0:NB], earlier[0:EP, 0:EP], cnt[:], start=True, stop=True)
            nc.tensor.matmul(ps_cnt[:, 16:16 + NB], ones[0:EP, 0:P], cnt[:], start=True, stop=True).then_inc(summed, 1)
            pe.wait_ge(w_in, 16)

            def place(c, j, start, stop):
                pe.wait_ge(operands, c + 1)
                nc.tensor.matmul(place_d[:, 0:NT], hot_lo_d[:, j % PR, :], hot_hi[:, j % PR, :],
                                 start=start, stop=stop)
                nc.tensor.matmul(place_s[:, 0:NT], hot_lo_s[:, j % PR, :], hot_hi[:, j % PR, :],
                                 start=start, stop=stop).then_inc(placed, 1)

            for g in range(NB):
                par = g % 2
                pe.wait_ge(h_ready, g + 1)
                if g >= 1:
                    pe.wait_ge(hT_ready, g)
                for c in range(KC):
                    last = nc.tensor.transpose(ps_hT[:, c * P:(c + 1) * P], h[:, par, c * P:(c + 1) * P], ident[:])
                last.then_inc(hT_done, 1)
                for j in range(CPB // 2):
                    place(g * CPB + j, j, g == 0 and j == 0, False)
                pe.wait_ge(hT_ready, g + 1)
                if g >= 1:
                    pe.wait_ge(u_biased, g)
                    pe.wait_ge(v_copied, g)
                for c in range(KC):
                    last = nc.tensor.matmul(ps_u[:], hT[:, par, c * P:(c + 1) * P], w_sb[:, c, :],
                                            start=(c == 0), stop=(c == KC - 1))
                last.then_inc(u_done, 1)
                for c in range(KC):
                    last = nc.tensor.matmul(ps_v[:], hT[:, par, c * P:(c + 1) * P], w_sb[:, KC + c, :],
                                            start=(c == 0), stop=(c == KC - 1))
                last.then_inc(v_done, 1)
                for j in range(CPB // 2, CPB):
                    place(g * CPB + j, j, False, g == NB - 1 and j == CPB - 1)

            pe.wait_ge(nodes_ready, 1)
            pe.wait_ge(groups_ready, 1)
            pe.wait_ge(u_low, NB)

            def turn(t, j):
                pe.wait_ge(hot_ready, t + 1)
                if not (isinstance(t, int) and t < 2):
                    pe.wait_ge(hotT_ready, t - 1)
                nc.tensor.transpose(ps_hotT[j % 2][:, 0:P], hot[:, j % R, :], ident[:]).then_inc(hotT_done, 1)

            turn(0, 0)
            cur = [None]

            def step(k, j, i):
                static = isinstance(k, int)
                if not static or k + 1 < NT:
                    turn(k + 1, j + 1)
                if not static or k < NT:
                    pe.wait_ge(hotT_ready, k + 1)
                    if not (static and k < R4):
                        pe.wait_ge(pre_ready, k - R4 + 1)
                    if j % 2 == 0:
                        s = k // 2 if static else i * (R // 2) + j // 2
                        cur[0] = pe.value_load(gb_i[0:1, bass.ds(s, 1)], min_val=0, max_val=NB - 1)
                    for part in range(3):
                        last = nc.tensor.matmul(ps_exp[j % R4][:], hotT[:, j % R4, :],
                                                u3[:, part, bass.ds(cur[0], 1), :].rearrange("p a d -> p (a d)"),
                                                start=(part == 0), stop=(part == 2))
                    last.then_inc(spread, 1)
                if not (static and k < 2):
                    t, jj = k - 2, (j - 2) % R
                    pe.wait_ge(msg_ready, t + 1)
                    if jj % 2 == 0 and not (static and t < 4):
                        s = t // 2 if static else i * (R // 2) + (j // 2 - 1)
                        pe.wait_ge(added, s - 1)
                    nc.tensor.matmul(ps_agg[(jj // 2) % 2][:], hot[:, jj, :], msg[:, jj % R4, :],
                                     start=(jj % 2 == 0), stop=(jj % 2 == 1)).then_inc(summed_tiles, 1)

            turns(pe, step, 0, NT + 2)


def kernel(**inputs):
    import numpy as np
    import concourse.bacc as bacc
    from concourse.bass_utils import run_bass_kernel_spmd

    nc = bacc.Bacc("TRN2", target_bir_lowering=False, num_devices=1)
    laid = {
        "x": np.ascontiguousarray(inputs["x"]),
        "src": np.ascontiguousarray(inputs["src"]),
        "dst": np.ascontiguousarray(inputs["dst"]),
        "wt": np.ascontiguousarray(np.asarray(inputs["L0_gnn_W"]).T),
        "bias": np.ascontiguousarray(inputs["L0_gnn_b"]),
    }
    args = {k: nc.dram_tensor(f"in_{k}", a.shape, mybir.dt.from_np(a.dtype), kind="ExternalInput").ap()
            for k, a in laid.items()}
    out = nc.dram_tensor("out_0", laid["x"].shape, F32, kind="ExternalOutput").ap()
    bass_gnn_edge_messages(nc, args["x"], args["src"], args["dst"], args["wt"], args["bias"], out)
    r = run_bass_kernel_spmd(nc, [{f"in_{k}": a for k, a in laid.items()}], core_ids=[0])
    return r.results[0]["out_0"]
```

```python
from contextlib import ExitStack

import concourse.bass as bass
from concourse import mybir

ALU = mybir.AluOpType
ACT = mybir.ActivationFunctionType
F32 = mybir.dt.float32
F16 = mybir.dt.float16
F32R = mybir.dt.float32r
I32 = mybir.dt.int32

P = 128
EPS = 1e-5
GROUP = 2


def bass_gnn_edge_messages(nc, x, src, dst, wt, bias, out):
    N, D = x.shape
    (E,) = src.shape
    KC = D // P
    NB = -(-N // P)
    LAST = N - (NB - 1) * P
    EP = max(p for p in range(1, P + 1) if E % p == 0)
    EC = E // EP
    GS = GROUP * P
    NG = (E + NB * (GS - 1)) // GS
    NT = NG * GROUP
    assert NT <= 512 and EC % NB == 0 and D == 512

    B = 8
    BATCHES = EC // B
    EARLY = 2
    PAIRS = (NB - EARLY) // 2
    BPT = BATCHES // PAIRS
    FIRST = BPT // 4 * 2
    R = 8
    FROM_DRAM = (3, 7)
    SPREAD = [j for j in range(R) if j not in FROM_DRAM]
    RA = len(SPREAD)
    M4, U3 = 4, 3
    TURNS = NT // R
    assert (NB - EARLY) % 2 == 0 and BATCHES % PAIRS == 0 and BPT % 2 == 0 and RA % (2 * U3) == 0

    v_rows = nc.dram_tensor("v_rows", [N, D], F32, kind="Internal").ap()
    u_rows = nc.dram_tensor("u_rows", [N, D], F32, kind="Internal").ap()

    with ExitStack() as ctx:
        def sb(name, shape, dt):
            return ctx.enter_context(nc.sbuf_tensor(name, shape, dt))

        def sem(name):
            return ctx.enter_context(nc.semaphore(name))

        bank = [ctx.enter_context(nc.psum_tensor(f"bank{i}", [P, 512], F32)) for i in range(8)]

        acc = sb("acc", [P, NB, D], F32)
        w_sb = sb("w_sb", [P, 2 * KC, D], F32)
        b_sb = sb("b_sb", [P, D], F32)
        iota1 = sb("iota1", [P, P], F32)
        iota16 = sb("iota16", [P, NT], F16)
        pcol = sb("pcol", [P, 1], F32)
        ident = sb("ident", [P, P], F32)
        earlier = sb("earlier", [P, P], F32)
        ones = sb("ones", [P, 512], F32)
        zeros = sb("zeros", [EP, P], F16)
        iota_b = sb("iota_b", [P, P, B], F16)
        group_no = sb("group_no", [P, NG], F32)
        eps_col = sb("eps_col", [P, 1], F32)

        src_i = sb("src_i", [EP, EC], I32)
        dst_i = sb("dst_i", [EP, EC], I32)
        tmp_i = sb("tmp_i", [EP, EC], I32)
        blk_i = sb("blk_i", [EP, EC], I32)
        blk_f = sb("blk_f", [EP, EC], F32)
        node1 = sb("node1", [EP, EC], F32)
        dst_h = sb("dst_h", [EP, EC], F16)
        cnt = sb("cnt", [EP, NB], F32)
        pos = sb("pos", [EP, EC], F32)
        pos_i = sb("pos_i", [EP, EC], I32)
        pos_hi_i = sb("pos_hi_i", [EP, EC], I32)
        pos_lo = sb("pos_lo", [EP, EC], F16)
        pos_hi = sb("pos_hi", [EP, EC], F32)
        tot_i = sb("tot_i", [P, NB], I32)
        ngr_i = sb("ngr_i", [P, NB], I32)
        ngr = sb("ngr", [P, NB], F32)
        g_end = sb("g_end", [P, NB], F32)
        g_start = sb("g_start", [P, NB], F32)
        off = sb("off", [P, NB], F32)
        gb_f = sb("gb_f", [P, NG], F32)
        gb_i = sb("gb_i", [1, NG], I32)

        stats = sb("stats", [P, NB, 6], F32)
        mv = sb("mv", [P, NB, 2], F32)
        std = sb("std", [P, NB], F32)
        rstd = sb("rstd", [P, NB], F32)
        nmr = sb("nmr", [P, NB], F32)
        h = sb("h", [P, 2, D], F32)
        hT = sb("hT", [P, 2, D], F32)
        v_out = sb("v_out", [P, 2, D], F32)
        u_f = sb("u_f", [P, 2, D], F32)
        u2 = sb("u2", [P, 2, NB, D], F32R)

        hot_lo = sb("hot_lo", [EP, 2, P, B], F16)
        hot_lo_d = sb("hot_lo_d", [EP, 2, P, B], F16)
        hot_lo_s = sb("hot_lo_s", [EP, 2, B, P], F16)
        hot_hi = sb("hot_hi", [EP, 2, B, NT], F16)

        slot_dst = sb("slot_dst", [P, NT + R], I32)
        slot_src = sb("slot_src", [P, NT + R], I32)
        slot_node1 = sb("slot_node1", [P, NT], F32)
        node0 = sb("node0", [P, NT], F32)
        window = sb("window", [P, R], I32)
        window_u = sb("window_u", [P, len(FROM_DRAM)], I32)
        v_t = sb("v_t", [P, R, D], F32)
        hot = sb("hot", [P, R, P], F32)
        hotT = sb("hotT", [P, U3, P], F32R)
        pre_msg = sb("pre_msg", [P, RA + M4, D], F32)
        pre, msg = pre_msg[:, 0:RA, :], pre_msg[:, RA:RA + M4, :]

        def edges_by_block(t):
            flat = t[0:EP].rearrange("p r d -> p (r d)")
            return flat[:, 0:NB * EC].rearrange("p (b c) -> p b c", b=NB)

        in_blk = edges_by_block(v_t)
        running = edges_by_block(pre_msg)

        place_d, place_s = bank[0], bank[1]
        ps_hT, ps_cnt = bank[2], bank[3]
        ps_u, ps_v = bank[4:6], bank[6:8]
        ps_spread = [bank[i] for i in (0, 1, 2)]
        ps_hotT = [bank[i] for i in (4, 5)]
        ps_agg = [bank[i] for i in (6, 7)]

        src_in, dst_in, b_in = sem("src_in"), sem("dst_in"), sem("b_in")
        w_in = [sem(f"w_in{i}") for i in range(2)]
        x_in = [sem(f"x_in{i}") for i in range(2)]
        rest_zero = sem("rest_zero")
        first_consts, consts = sem("first_consts"), sem("consts")
        masks = sem("masks")
        dve_step = sem("dve_step")
        counted, summed = sem("counted"), sem("summed")
        mv_ready, std_ready, norm_ready = sem("mv_ready"), sem("std_ready"), sem("norm_ready")
        h_ready, hT_done, hT_ready = sem("h_ready"), sem("hT_done"), sem("hT_ready")
        u_done, v_done = sem("u_done"), sem("v_done")
        u_biased, u_high, u_low = sem("u_biased"), sem("u_high"), sem("u_low")
        v_copied = sem("v_copied")
        v_stored = [sem(f"v_stored{i}") for i in range(2)]
        u_stored = [sem(f"u_stored{i}") for i in range(2)]
        room = sem("room")
        lo_ready, operands_d, operands_s = sem("lo_ready"), sem("operands_d"), sem("operands_s")
        tables, nodes_ready, src_table = sem("tables"), sem("nodes_ready"), sem("src_table")
        groups_ready = sem("groups_ready")
        window_ready = sem("window_ready")
        v_landed = [sem(f"v_landed{i}") for i in range(R)]
        uv_landed = [sem(f"uv_landed{i}") for i in range(len(FROM_DRAM))]
        hot_ready, hotT_done, hotT_ready = sem("hot_ready"), sem("hotT_done"), sem("hotT_ready")
        spread, pre_ready, msg_ready = sem("spread"), sem("pre_ready"), sem("msg_ready")
        slot_free = sem("slot_free")
        gathers_let = sem("gathers_let")
        summed_tiles, added = sem("summed_tiles"), sem("added")
        out_stored = sem("out_stored")

        def tile(i, j):
            return i * R + j

        def nth_spread(i, j):
            return (i + j // R) * RA + SPREAD.index(j % R)

        def is_spread(j):
            return j % R in SPREAD

        def exists(i, j):
            return not isinstance(i, int) or 0 <= tile(i, j) < NT

        def at_least(i, j, n):
            return not isinstance(i, int) or tile(i, j) >= n

        def turns(eng, step, steps):
            for j in range(R):
                step(0, j)
            with eng.Fori(1, TURNS) as i:
                for j in range(R):
                    step(i, j)
            for k in range(TURNS * R, steps):
                step(k // R, k % R)

        def is_block(g):
            return not isinstance(g, int) or g < NB

        def prepare_turns(eng, block_work, batch, ahead=False, between=None):
            def turn(o):
                for par in range(2):
                    own = range(FIRST) if par == 0 else range(FIRST, BPT)
                    if ahead:
                        block_work(o * 2 + EARLY + par, par, o)
                    for m in own:
                        batch(o * BPT + m, m % 2)
                        if m == own[1] and not ahead:
                            block_work(o * 2 + EARLY + par, par, o)

            with eng.Fori(0, PAIRS - 1) as o:
                turn(o)
            if between is not None:
                between()
            turn(PAIRS - 1)

        block = ctx.enter_context(nc.Block())

        @block.sync
        def _(sp):
            sp.dma_start(acc[:, 0:EARLY, :], x[0:EARLY * P, :].rearrange("(b p) d -> p b d", p=P)).then_inc(x_in[0], 16)
            sp.dma_start(src_i[:], src.rearrange("(p c) -> p c", p=EP)).then_inc(src_in, 16)
            for part in range(2):
                sp.dma_start(w_sb[:, part * KC:(part + 1) * KC, :],
                             wt[part * D:(part + 1) * D, :].rearrange("(c p) o -> p c o", p=P)).then_inc(w_in[part], 16)
            sp.dma_start(acc[:, EARLY:NB - 1, :],
                         x[EARLY * P:(NB - 1) * P, :].rearrange("(b p) d -> p b d", p=P)).then_inc(x_in[1], 16)
            sp.wait_ge(rest_zero, 1)
            sp.dma_start(acc[0:LAST, NB - 1, :], x[(NB - 1) * P:N, :]).then_inc(x_in[1], 16)
            sp.dma_start(dst_i[:], dst.rearrange("(p c) -> p c", p=EP)).then_inc(dst_in, 16)
            sp.dma_start(b_sb[:], bias.rearrange("(a d) -> a d", a=1).to_broadcast([P, D])).then_inc(b_in, 16)
            for g in range(NB):
                rows = P if g < NB - 1 else LAST
                sp.wait_ge(v_copied, g + 1)
                sp.dma_start(v_rows[g * P:g * P + rows, :], v_out[0:rows, g % 2, :]).then_inc(v_stored[g % 2], 16)
                sp.wait_ge(u_biased, g + 1)
                sp.dma_start(u_rows[g * P:g * P + rows, :], u_f[0:rows, g % 2, :]).then_inc(u_stored[g % 2], 16)
            sp.wait_ge(added, NG)
            sp.dma_start(out[0:(NB - 1) * P, :].rearrange("(b p) d -> p b d", p=P),
                         acc[:, 0:NB - 1, :]).then_inc(out_stored, 16)
            sp.dma_start(out[(NB - 1) * P:N, :], acc[0:LAST, NB - 1, :]).then_inc(out_stored, 16)
            sp.wait_ge(out_stored, 32)

        @block.gpsimd
        def _(pool):
            nc.gpsimd.iota(iota1[:], pattern=[[1, P]], base=1, channel_multiplier=0,
                           allow_small_or_imprecise_dtypes=True).then_inc(first_consts, 1)
            nc.gpsimd.iota(pcol[:], pattern=[[1, 1]], base=1, channel_multiplier=1,
                           allow_small_or_imprecise_dtypes=True).then_inc(first_consts, 1)
            nc.gpsimd.memset(acc[:, NB - 1, :], 0.0).then_inc(rest_zero, 1)
            nc.gpsimd.memset(zeros[:], 0.0).then_inc(consts, 1)
            nc.gpsimd.iota(iota16[:], pattern=[[1, NT]], base=0, channel_multiplier=0,
                           allow_small_or_imprecise_dtypes=True).then_inc(consts, 1)
            nc.gpsimd.iota(iota_b[:], pattern=[[1, P], [0, B]], base=0, channel_multiplier=0,
                           allow_small_or_imprecise_dtypes=True).then_inc(consts, 1)
            nc.gpsimd.iota(group_no[:], pattern=[[1, NG]], base=0, channel_multiplier=0,
                           allow_small_or_imprecise_dtypes=True).then_inc(consts, 1)
            for g in range(NB):
                pool.wait_ge(u_high, g + 1)
                nc.gpsimd.tensor_tensor(u2[:, 1, g, :], u_f[:, g % 2, :], u2[:, 0, g, :],
                                        ALU.subtract).then_inc(u_low, 1)
            for par in range(2):
                pool.wait_ge(v_stored[par], 16 * ((NB + 1 - par) // 2))
                pool.wait_ge(u_stored[par], 16 * ((NB + 1 - par) // 2))
            pool.wait_ge(window_ready, 1)

            def step(i, j):
                if exists(i, j):
                    if at_least(i, j, R):
                        pool.wait_ge(slot_free, tile(i, j) - R + 1)
                        pool.sem_inc(gathers_let, 1)
                    nc.gpsimd.indirect_dma_start(
                        out=v_t[:, j, :], out_offset=None, in_=v_rows,
                        in_offset=bass.IndirectOffsetOnAxis(ap=window[:, j:j + 1], axis=0),
                    ).then_inc(v_landed[j], 16)
                if not is_spread(j - 3) and exists(i, j - 3) and at_least(i, j - 3, 0):
                    jj = (j - 3) % R
                    n = FROM_DRAM.index(jj)
                    if not at_least(i, j - 3, R):
                        pool.wait_ge(window_ready, 2)
                    pool.wait_ge(v_landed[jj], 16 * (i + (j - 3) // R + 1))
                    pool.sem_inc(gathers_let, 1)
                    nc.gpsimd.indirect_dma_start(
                        out=v_t[:, jj, :], out_offset=None, in_=u_rows,
                        in_offset=bass.IndirectOffsetOnAxis(ap=window_u[:, n:n + 1], axis=0),
                        compute_op=ALU.add,
                    ).then_inc(uv_landed[n], 16)

            turns(pool, step, NT + 3)

        @block.vector
        def _(dve):
            chain = [0]

            def link(ins):
                chain[0] += 1
                ins.then_inc(dve_step, 1)
                dve.wait_ge(dve_step, chain[0])

            def statistics(first, last, part):
                dve.wait_ge(x_in[part], 16 if part == 0 else 32)
                for b in range(first, last):
                    rows = P if b < NB - 1 else LAST
                    ins = nc.vector.bn_stats(stats[0:rows, b, :], acc[0:rows, b, :])
                link(ins)
                for b in range(first, last):
                    rows = P if b < NB - 1 else LAST
                    ins = nc.vector.bn_aggr(mv[0:rows, b, :], stats[0:rows, b, :])
                ins.then_inc(mv_ready, 1)

            def norms(first, last, part):
                dve.wait_ge(std_ready, part + 1)
                link(nc.vector.reciprocal(rstd[:, first:last], std[:, first:last]))
                nc.vector.scalar_tensor_tensor(nmr[:, first:last], mv[:, first:last, 0], -1.0, rstd[:, first:last],
                                               ALU.mult, ALU.mult).then_inc(norm_ready, 1)

            nc.vector.memset(ones[:], 1.0)
            nc.vector.memset(eps_col[:], EPS)
            nc.vector.memset(mv[:, NB - 1, :], 0.0)
            nc.vector.memset(slot_dst[:, NT:NT + R], 0)
            nc.vector.memset(slot_src[:, NT:NT + R], 0)
            dve.wait_ge(first_consts, 2)
            nc.vector.tensor_scalar(ident[:], iota1[:], pcol[:], None, ALU.is_equal)
            nc.vector.tensor_scalar(earlier[:], iota1[:], pcol[:], None, ALU.is_gt).then_inc(masks, 1)
            statistics(0, EARLY, 0)

            dve.wait_ge(src_in, 16)
            nc.vector.tensor_scalar(blk_i[:], src_i[:], 7, None, ALU.arith_shift_right)
            link(nc.vector.tensor_scalar(tmp_i[:], src_i[:], P - 1, None, ALU.bitwise_and))
            norms(0, EARLY, 0)
            nc.vector.tensor_scalar(node1[:], tmp_i[:], 1.0, None, ALU.add)
            link(nc.vector.tensor_copy(blk_f[:], blk_i[:]))
            for b in range(NB):
                last = nc.vector.tensor_scalar(in_blk[:, b, :], blk_f[:], float(b), None, ALU.is_equal)
            link(last)
            for b in range(NB):
                last = nc.vector.tensor_tensor_scan(running[:, b, :], ones[0:EP, 0:EC], in_blk[:, b, :],
                                                    0.0, ALU.mult, ALU.add)
            link(last)
            nc.vector.tensor_copy(cnt[:], running[:, :, EC - 1]).then_inc(counted, 1)
            statistics(EARLY, NB, 1)

            dve.wait_ge(summed, 1)
            link(nc.vector.tensor_scalar(tot_i[:], ps_cnt[:, 16:16 + NB], float(GS - 1), None, ALU.add))
            link(nc.vector.tensor_scalar(ngr_i[:], tot_i[:], GS.bit_length() - 1, None, ALU.arith_shift_right))
            link(nc.vector.tensor_copy(ngr[:], ngr_i[:]))
            link(nc.vector.tensor_tensor_scan(g_end[:], ones[:, 0:NB], ngr[:], 0.0, ALU.mult, ALU.add))
            link(nc.vector.tensor_tensor(g_start[:], g_end[:], ngr[:], ALU.subtract))
            link(nc.vector.tensor_scalar(off[:], g_start[:], float(GS), -1.0, ALU.mult, ALU.add))
            link(nc.vector.tensor_tensor(off[0:EP, :], off[0:EP, :], ps_cnt[0:EP, 0:NB], ALU.add))
            for b in range(NB):
                last = nc.vector.scalar_tensor_tensor(running[:, b, :], running[:, b, :], off[0:EP, b:b + 1],
                                                      in_blk[:, b, :], ALU.add, ALU.mult)
            link(last)
            norms(EARLY, NB, 1)
            link(nc.vector.tensor_reduce(pos[:], running[:].rearrange("p b c -> p c b"),
                                         mybir.AxisListType.X, ALU.add))
            link(nc.vector.tensor_copy(pos_i[:], pos[:]))
            nc.vector.tensor_scalar(pos_hi_i[:], pos_i[:], 7, None, ALU.arith_shift_right)
            link(nc.vector.tensor_scalar(tmp_i[:], pos_i[:], P - 1, None, ALU.bitwise_and))
            nc.vector.tensor_copy(pos_lo[:], tmp_i[:])
            nc.vector.tensor_copy(pos_hi[:], pos_hi_i[:])
            dve.wait_ge(dst_in, 16)
            link(nc.vector.tensor_copy(dst_h[:], dst_i[:]))
            dve.wait_ge(b_in, 16)

            def bias_u(g, par, o):
                dve.wait_ge(u_done, g + 1)
                if o is not None:
                    dve.wait_ge(u_low, g - 1)
                    dve.wait_ge(u_stored[par], 16 * (o + 1))
                nc.vector.tensor_tensor(u_f[:, par, :], ps_u[par][:], b_sb[:], ALU.add).then_inc(u_biased, 1)

            bias_u(0, 0, None)
            bias_u(1, 1, None)
            dve.wait_ge(consts, 4)

            def group_blocks():
                link(nc.vector.tensor_scalar(gb_f[:], group_no[:], g_end[:, 0:1], None, ALU.is_ge))
                for b in range(1, NB - 1):
                    link(nc.vector.scalar_tensor_tensor(gb_f[:], group_no[:], g_end[:, b:b + 1], gb_f[:],
                                                        ALU.is_ge, ALU.add))
                nc.vector.tensor_copy(gb_i[:], gb_f[0:1, :]).then_inc(groups_ready, 1)

            def batch(m, par):
                dve.wait_ge(room, m + 1)
                cols = bass.ds(m * B, B)
                def over_slots(t):
                    return t[:, cols].rearrange("p (a c) -> p a c", a=1).to_broadcast([EP, P, B])
                nc.vector.tensor_tensor(hot_lo[:, par], iota_b[0:EP], over_slots(pos_lo),
                                        ALU.is_equal).then_inc(lo_ready, 1)
                for c in range(B):
                    nc.vector.tensor_scalar(hot_hi[:, par, c, :], iota16[0:EP, :], pos_hi[:, bass.ds(m * B + c, 1)],
                                            None, ALU.is_equal)
                dve.wait_ge(lo_ready, m + 1)
                nc.vector.tensor_tensor(hot_lo_d[:, par], hot_lo[:, par], over_slots(dst_h),
                                        ALU.mult).then_inc(operands_d, 1)

            prepare_turns(dve, bias_u, batch, between=group_blocks)

            dve.wait_ge(room, BATCHES + 2)
            nc.vector.tensor_copy(slot_dst[:, 0:NT], place_d[:, 0:NT]).then_inc(tables, 1)
            nc.vector.tensor_copy(slot_node1[:], place_s[:, 0:NT]).then_inc(nodes_ready, 1)
            dve.wait_ge(nodes_ready, 1)
            link(nc.vector.tensor_scalar(node0[:], slot_node1[:], -1.0, 0.0, ALU.add, ALU.max))
            nc.vector.scalar_tensor_tensor(
                slot_src[:, 0:NT].rearrange("p (g t) -> p g t", t=GROUP),
                gb_f[:].rearrange("p (g a) -> p g a", a=1).to_broadcast([P, NG, GROUP]), float(P),
                node0[:].rearrange("p (g t) -> p g t", t=GROUP), ALU.mult, ALU.add).then_inc(src_table, 1)

            def one_hot(i, j):
                if at_least(i, j, R):
                    dve.wait_ge(summed_tiles, tile(i, j) - R + 1)
                nc.vector.tensor_scalar(hot[:, j % R, :], iota1[:], slot_node1[:, bass.ds(tile(i, j), 1)], None,
                                        ALU.is_equal).then_inc(hot_ready, 1)

            for j in range(3):
                one_hot(0, j)

            def step(i, j):
                if is_spread(j) and exists(i, j):
                    n = SPREAD.index(j)
                    dve.wait_ge(v_landed[j], 16 * (i + 1))
                    dve.wait_ge(spread, nth_spread(i, j) + 1)
                    nc.vector.tensor_tensor(pre[:, n, :], v_t[:, j, :], ps_spread[n % U3][:],
                                            ALU.add).then_inc(pre_ready, 1)
                if exists(i, j + 3):
                    one_hot(i, j + 3)
                if j % GROUP == 0 and at_least(i, j, 2 * GROUP):
                    s = i * (R // GROUP) + (j // GROUP - 2)
                    dve.wait_ge(summed_tiles, s * GROUP + GROUP)
                    if at_least(i, j, 2 * GROUP + 1):
                        dve.wait_ge(added, s)
                    b = dve.value_load(gb_i[0:1, bass.ds(s, 1)], min_val=0, max_val=NB - 1)
                    a = acc[:, bass.ds(b, 1), :].rearrange("p a d -> p (a d)")
                    nc.vector.tensor_tensor(a, a, ps_agg[(j // GROUP) % 2][:], ALU.add).then_inc(added, 1)

            turns(dve, step, NT + 3)

        @block.scalar
        def _(act):
            def normalize(g, par):
                nc.scalar.activation(h[:, par, :], acc[:, bass.ds(g, 1), :].rearrange("p a d -> p (a d)"),
                                     ACT.Relu, bias=nmr[:, bass.ds(g, 1)],
                                     scale=rstd[:, bass.ds(g, 1)]).then_inc(h_ready, 1)

            def turned_h(g, par):
                act.wait_ge(hT_done, g + 1)
                nc.scalar.copy(hT[:, par, :], ps_hT[:]).then_inc(hT_ready, 1)

            def parts(g, par, o):
                act.wait_ge(v_done, g + 1)
                if o is not None:
                    act.wait_ge(v_stored[par], 16 * (o + 1))
                nc.scalar.copy(v_out[:, par, :], ps_v[par][:]).then_inc(v_copied, 1)
                act.wait_ge(u_biased, g + 1)
                nc.scalar.copy(u2[:, 0, bass.ds(g, 1), :].rearrange("p a d -> p (a d)"),
                               u_f[:, par, :]).then_inc(u_high, 1)

            act.wait_ge(mv_ready, 1)
            nc.scalar.activation(std[:, 0:EARLY], mv[:, 0:EARLY, 1], ACT.Sqrt, bias=eps_col[:]).then_inc(std_ready, 1)
            act.wait_ge(norm_ready, 1)
            for g in range(EARLY):
                normalize(g, g)
            turned_h(0, 0)
            turned_h(1, 1)
            act.wait_ge(mv_ready, 2)
            nc.scalar.activation(std[:, EARLY:NB], mv[:, EARLY:NB, 1], ACT.Sqrt,
                                 bias=eps_col[:]).then_inc(std_ready, 1)
            act.wait_ge(norm_ready, 2)
            normalize(2, 0)
            normalize(3, 1)
            act.wait_ge(v_done, 1)
            turned_h(2, 0)
            parts(0, 0, None)
            parts(1, 1, None)

            def block_work(g, par, o):
                parts(g, par, o)
                if is_block(g + 1):
                    turned_h(g + 1, 1 - par)
                if is_block(g + 2):
                    normalize(g + 2, par)

            def batch(m, par):
                act.wait_ge(lo_ready, m + 1)
                for c in range(B):
                    ins = nc.scalar.activation(hot_lo_s[:, par, c, :], hot_lo[:, par, :, c], ACT.Copy,
                                               scale=node1[:, bass.ds(m * B + c, 1)])
                ins.then_inc(operands_s, 1)

            prepare_turns(act, block_work, batch)

            act.wait_ge(tables, 1)
            nc.scalar.copy(window[:], slot_dst[:, 0:R]).then_inc(window_ready, 1)
            act.wait_ge(src_table, 1)
            for n, j in enumerate(FROM_DRAM):
                ins = nc.scalar.copy(window_u[:, n:n + 1], slot_src[:, j:j + 1])
            ins.then_inc(window_ready, 1)

            def turned(i, j):
                n = SPREAD.index(j % R)
                act.wait_ge(hotT_done, nth_spread(i, j) + 1)
                nc.scalar.copy(hotT[:, n % U3, :], ps_hotT[n % 2][:, 0:P]).then_inc(hotT_ready, 1)

            turned(0, 0)

            def step(i, j):
                if is_spread(j + 1) and exists(i, j + 1):
                    turned(i, j + 1)
                if is_spread(j):
                    act.wait_ge(pre_ready, nth_spread(i, j) + 1)
                    taken = pre[:, SPREAD.index(j), :]
                else:
                    act.wait_ge(uv_landed[FROM_DRAM.index(j)], 16 * (i + 1))
                    taken = v_t[:, j, :]
                if at_least(i, j, M4):
                    act.wait_ge(summed_tiles, tile(i, j) - M4 + 1)
                nc.scalar.activation(msg[:, j % M4, :], taken, ACT.Relu).then_inc(msg_ready, 1)
                if not is_spread(j):
                    n = FROM_DRAM.index(j)
                    nc.scalar.copy(window_u[:, n:n + 1], slot_src[:, bass.ds(tile(i, j) + R, 1)])
                nc.scalar.copy(window[:, j:j + 1], slot_dst[:, bass.ds(tile(i, j) + R, 1)]).then_inc(slot_free, 1)

            turns(act, step, NT)

        @block.tensor
        def _(pe):
            def turn_h(g, par):
                pe.wait_ge(h_ready, g + 1)
                for c in range(KC):
                    last = nc.tensor.transpose(ps_hT[:, c * P:(c + 1) * P], h[:, par, c * P:(c + 1) * P], ident[:])
                last.then_inc(hT_done, 1)

            def product(g, par, o):
                pe.wait_ge(hT_ready, g + 1)
                if o is not None:
                    pe.wait_ge(u_biased, g - 1)
                else:
                    pe.wait_ge(w_in[0], 16)
                for c in range(KC):
                    last = nc.tensor.matmul(ps_u[par][:], hT[:, par, c * P:(c + 1) * P], w_sb[:, c, :],
                                            start=(c == 0), stop=(c == KC - 1))
                last.then_inc(u_done, 1)
                if o is not None:
                    pe.wait_ge(v_copied, g - 1)
                else:
                    pe.wait_ge(w_in[1], 16)
                for c in range(KC):
                    last = nc.tensor.matmul(ps_v[par][:], hT[:, par, c * P:(c + 1) * P], w_sb[:, KC + c, :],
                                            start=(c == 0), stop=(c == KC - 1))
                last.then_inc(v_done, 1)

            pe.sem_inc(room, 2)
            pe.wait_ge(masks, 1)
            turn_h(0, 0)
            pe.wait_ge(hT_ready, 1)
            turn_h(1, 1)
            product(0, 0, None)
            pe.wait_ge(counted, 1)
            nc.tensor.matmul(ps_cnt[0:EP, 0:NB], earlier[0:EP, 0:EP], cnt[:], start=True, stop=True)
            nc.tensor.matmul(ps_cnt[:, 16:16 + NB], ones[0:EP, 0:P], cnt[:], start=True, stop=True).then_inc(summed, 1)
            product(1, 1, None)
            turn_h(2, 0)

            pe.wait_ge(consts, 2)
            for table in (place_d, place_s):
                nc.tensor.matmul(table[:, 0:NT], zeros[:], iota16[0:EP, :], start=True, stop=False,
                                 skip_group_check=True)

            def block_work(g, par, o):
                product(g, par, o)
                if is_block(g + 1):
                    turn_h(g + 1, 1 - par)

            def batch(m, par):
                pe.wait_ge(operands_d, m + 1)
                pe.wait_ge(operands_s, m + 1)
                for c in range(B):
                    end = isinstance(m, int) and m == BATCHES - 1 and c == B - 1
                    nc.tensor.matmul(place_d[:, 0:NT], hot_lo_d[:, par, :, c], hot_hi[:, par, c, :],
                                     start=False, stop=end, skip_group_check=True)
                    last = nc.tensor.matmul(place_s[:, 0:NT], hot_lo_s[:, par, c, :], hot_hi[:, par, c, :],
                                            start=False, stop=end, skip_group_check=True)
                last.then_inc(room, 1)

            prepare_turns(pe, block_work, batch, ahead=True)

            pe.wait_ge(nodes_ready, 1)
            pe.wait_ge(groups_ready, 1)
            pe.wait_ge(u_low, NB)
            group_block = [None]

            def turn_hot(i, j):
                n = SPREAD.index(j % R)
                pe.wait_ge(hot_ready, tile(i, j) + 1)
                nc.tensor.transpose(ps_hotT[n % 2][:, 0:P], hot[:, j % R, :], ident[:]).then_inc(hotT_done, 1)

            turn_hot(0, 0)
            turn_hot(0, 1)

            def step(i, j):
                if exists(i, j):
                    if j % GROUP == 0:
                        group_block[0] = pe.value_load(gb_i[0:1, bass.ds(i * (R // GROUP) + j // GROUP, 1)],
                                                       min_val=0, max_val=NB - 1)
                    if is_spread(j):
                        n = SPREAD.index(j)
                        pe.wait_ge(hotT_ready, nth_spread(i, j) + 1)
                        for part in range(2):
                            last = nc.tensor.matmul(
                                ps_spread[n % U3][:], hotT[:, n % U3, :],
                                u2[:, part, bass.ds(group_block[0], 1), :].rearrange("p a d -> p (a d)"),
                                start=(part == 0), stop=(part == 1))
                        last.then_inc(spread, 1)
                if is_spread(j + 2) and exists(i, j + 2):
                    turn_hot(i, j + 2)
                if at_least(i, j, 2):
                    t = (j - 2) % R
                    if t % GROUP == 0 and not exists(i, j + 2):
                        pe.wait_ge(added, (tile(i, j) - 2) // GROUP - 1)
                    pe.wait_ge(msg_ready, tile(i, j) - 1)
                    nc.tensor.matmul(ps_agg[(t // GROUP) % 2][:], hot[:, t, :], msg[:, t % M4, :],
                                     start=(t % GROUP == 0), stop=(t % GROUP == GROUP - 1)).then_inc(summed_tiles, 1)

            turns(pe, step, NT + 2)


def kernel(**inputs):
    import numpy as np
    import concourse.bacc as bacc
    from concourse.bass_utils import run_bass_kernel_spmd

    nc = bacc.Bacc("TRN2", target_bir_lowering=False, num_devices=1)
    laid = {
        "x": np.ascontiguousarray(inputs["x"]),
        "src": np.ascontiguousarray(inputs["src"]),
        "dst": np.ascontiguousarray(inputs["dst"]),
        "wt": np.ascontiguousarray(np.asarray(inputs["L0_gnn_W"]).T),
        "bias": np.ascontiguousarray(inputs["L0_gnn_b"]),
    }
    args = {k: nc.dram_tensor(f"in_{k}", a.shape, mybir.dt.from_np(a.dtype), kind="ExternalInput").ap()
            for k, a in laid.items()}
    out = nc.dram_tensor("out_0", laid["x"].shape, F32, kind="ExternalOutput").ap()
    bass_gnn_edge_messages(nc, args["x"], args["src"], args["dst"], args["wt"], args["bias"], out)
    r = run_bass_kernel_spmd(nc, [{f"in_{k}": a for k, a in laid.items()}], core_ids=[0])
    return r.results[0]["out_0"]
```

```python
from contextlib import ExitStack

import concourse.bass as bass
from concourse import mybir

ALU = mybir.AluOpType
ACT = mybir.ActivationFunctionType
F32 = mybir.dt.float32
F16 = mybir.dt.float16
BF16 = mybir.dt.bfloat16
F32R = mybir.dt.float32r
I32 = mybir.dt.int32

P = 128
EPS = 1e-5
GROUP = 2


def bass_gnn_edge_messages(nc, x, src, dst, wt, bias, out):
    N, D = x.shape
    (E,) = src.shape
    KC = D // P
    NB = -(-N // P)
    LAST = N - (NB - 1) * P
    EP = max(p for p in range(1, P + 1) if E % p == 0)
    EC = E // EP
    GS = GROUP * P
    NG = (E + NB * (GS - 1)) // GS
    NT = NG * GROUP
    assert NT <= 512 and EC % NB == 0 and D == 512 and N <= 2048

    FRACTION, BIAS = 23, 127
    NODE_EXP = BIAS - P // 2
    LOW = 10

    B = 8
    BATCHES = EC // B
    RB = 5
    EARLY = 2
    PAIRS = (NB - EARLY) // 2
    BPT = BATCHES // PAIRS
    FIRST = BPT // 4 * 2

    RG = 8
    RA = 4
    RK = 2
    WG = 2
    T = 8
    TURNS = NG // T
    HOT_AHEAD = 2
    GATHER_AHEAD = 2
    RELU_LAG = 3
    SPLIT_LAG = 4
    SUM_LAG = 5
    ADD_LAG = 6
    assert GROUP == 2 and RG % 2 == 0 and T % RG == 0 and T % (2 * RK) == 0 and T % (2 * RA) == 0 and RG % WG == 0
    assert NG % WG == 0 and 2 * RA <= 2 * KC
    assert (NB - EARLY) % 2 == 0 and BATCHES % PAIRS == 0 and BPT % RB == 0

    v_rows = nc.dram_tensor("v_rows", [N, D], F32, kind="Internal").ap()

    with ExitStack() as ctx:
        def sb(name, shape, dt):
            return ctx.enter_context(nc.sbuf_tensor(name, shape, dt))

        def sem(name):
            return ctx.enter_context(nc.semaphore(name))

        bank = [ctx.enter_context(nc.psum_tensor(f"bank{i}", [P, 512], F32)) for i in range(8)]

        acc = sb("acc", [P, NB, D], F32)
        w_sb = sb("w_sb", [P, 2 * KC, D], F32)
        b_sb = sb("b_sb", [P, D], F32)
        iota1 = sb("iota1", [P, P], F32)
        iota16 = sb("iota16", [P, NT], F16)
        pcol = sb("pcol", [P, 1], F32)
        ident = sb("ident", [P, P], F32)
        earlier = sb("earlier", [P, P], F32)
        ones = sb("ones", [P, EC], F32)
        zeros = sb("zeros", [EP, P], F16)
        iota_b = sb("iota_b", [P, P, B], F16)
        group_no = sb("group_no", [1, NG], F32)
        eps_col = sb("eps_col", [P, 1], F32)

        src_i = sb("src_i", [EP, EC], I32)
        dst_i = sb("dst_i", [EP, EC], I32)
        tmp_i = sb("tmp_i", [EP, EC], I32)
        over = sb("over", [EP, EC], F32)
        blk_i = sb("blk_i", [EP, EC], I32)
        node_exp = sb("node_exp", [EP, EC], I32)
        sign = sb("sign", [EP, EC], F32)
        dst_frac = sb("dst_frac", [EP, EC], F32)
        cnt = sb("cnt", [EP, NB], F32)
        pos = sb("pos", [EP, EC], F32)
        blk_f = pos
        pos_i = sb("pos_i", [EP, EC], I32)
        pos_lo = sb("pos_lo", [EP, EC], F16)
        pos_hi = sb("pos_hi", [EP, EC], F32)
        tot_i = sb("tot_i", [P, NB], I32)
        ngr_i = sb("ngr_i", [P, NB], I32)
        ngr = sb("ngr", [P, NB], F32)
        g_end = sb("g_end", [P, NB], F32)
        g_start = sb("g_start", [P, NB], F32)
        off = sb("off", [P, NB], F32)
        ended = sb("ended", [1, NG], F32)
        gb_f = sb("gb_f", [1, NG], F32)
        gb_i = sb("gb_i", [1, NG], I32)
        end_i = sb("end_i", [1, NB], I32)

        stats = sb("stats", [P, NB, 6], F32)
        mv = sb("mv", [P, NB, 2], F32)
        std = sb("std", [P, NB], F32)
        rstd = sb("rstd", [P, NB], F32)
        nmr = sb("nmr", [P, NB], F32)
        h = sb("h", [P, 2, D], F32)
        hT = sb("hT", [P, 2, D], F32)
        v_out = sb("v_out", [P, 2, D], F32)
        u_f = sb("u_f", [P, 2, D], F32)
        u2 = sb("u2", [P, 2, NB, D], F32R)

        hot_lo = sb("hot_lo", [EP, RB, P, B], F16)
        hot_lo_d = sb("hot_lo_d", [EP, RB, B, P], F16)

        slot_dst = sb("slot_dst", [P, NT], I32)
        slot_node1 = sb("slot_node1", [P, NT], F32)
        window = sb("window", [P, RG * GROUP], I32)
        ident_r = sb("ident_r", [P, P], F32R)
        hot = sb("hot", [P, RG, GROUP, P], F32R)
        hotT = sb("hotT", [P, 2, GROUP, P], F32R)
        ring = sb("ring", [P, max(RG * GROUP * D * 4, RB * B * NT * 2, 2 * NB * EC * 4) // 4], F32)
        v_t = ring[:, 0:RG * GROUP * D].rearrange("p (r t d) -> p r t d", t=GROUP, d=D)
        odd_high, odd_low = (sb(n, [P, 2 * RK, D], F32R) for n in ("odd_high", "odd_low"))
        even_high, even_low = (sb(n, [P, RK, D], F32R) for n in ("even_high", "even_low"))
        pre, msg = w_sb[:, 0:RA, :], w_sb[:, RA:2 * RA, :]

        flat = ring[0:EP, :]
        in_blk, running = (flat[:, n * NB * EC:(n + 1) * NB * EC].rearrange("p (b c) -> p b c", b=NB)
                           for n in range(2))
        hot_hi = flat.bitcast(BF16)[:, 0:RB * B * NT].rearrange("p (m c t) -> p m c t", m=RB, c=B)
        node_bits, low_bits, high_bits = (
            ring[:, RG * GROUP * D - (n + 1) * NT:RG * GROUP * D - n * NT].bitcast(I32) for n in range(3))

        place = bank[0]
        ps_hT, ps_cnt = bank[2], bank[3]
        ps_u, ps_v = bank[4:6], bank[6:8]
        ps_agg, ps_hotT, ps_spread = bank[0:2], bank[2:4], bank[4:8]

        src_in, dst_in, b_in = sem("src_in"), sem("dst_in"), sem("b_in")
        w_in = [sem(f"w_in{i}") for i in range(2)]
        x_in = [sem(f"x_in{i}") for i in range(2)]
        rest_zero = sem("rest_zero")
        first_consts, consts = sem("first_consts"), sem("consts")
        masks = sem("masks")
        dve_step = sem("dve_step")
        counted, summed = sem("counted"), sem("summed")
        mv_ready, std_ready, norm_ready = sem("mv_ready"), sem("std_ready"), sem("norm_ready")
        h_ready, hT_done, hT_ready = sem("h_ready"), sem("hT_done"), sem("hT_ready")
        u_done, v_done = sem("u_done"), sem("v_done")
        u_biased, u_high, u_low = sem("u_biased"), sem("u_high"), sem("u_low")
        v_copied = sem("v_copied")
        v_stored = [sem(f"v_stored{i}") for i in range(2)]
        room = sem("room")
        dst_step, dst_ready = sem("dst_step"), sem("dst_ready")
        lo_ready, operands_hi, operands_lo = sem("lo_ready"), sem("operands_hi"), sem("operands_lo")
        heads_ready, tables_ready, groups_ready = sem("heads_ready"), sem("tables_ready"), sem("groups_ready")
        pool_step, ends_ready = sem("pool_step"), sem("ends_ready")
        window_ready = sem("window_ready")
        v_landed = [[sem(f"v_landed{r}_{t}") for t in range(GROUP)] for r in range(RG)]
        hot_ready, hotT_done, hotT_ready = sem("hot_ready"), sem("hotT_done"), sem("hotT_ready")
        spread = [sem(f"spread{t}") for t in range(GROUP)]
        u_placed = [sem(f"u_placed{t}") for t in range(GROUP)]
        pre_ready = sem("pre_ready")
        msg_ready = [sem(f"msg_ready{t}") for t in range(GROUP)]
        split_ready = [sem(f"split_ready{t}") for t in range(GROUP)]
        gathers_let = sem("gathers_let")
        summed_groups, added = sem("summed_groups"), sem("added")
        out_stored = sem("out_stored")

        def nth(i, j):
            return i * T + j

        def nth_of_kind(i, j):
            return i * (T // 2) + j // 2

        def nth_in_place(i, j):
            return i * (T // RG) + j // RG + 1

        def is_placed(j, t):
            return t == 0 or j % 2 == 1

        def is_split(j, t):
            return t == 1 or j % 2 == 1

        def rows_of(j, t):
            return v_t[:, j % RG, t, :] if is_placed(j, t) else pre[:, j // 2 % RA, :]

        def parts_of(j, t):
            if t == 1:
                return odd_high[:, j % (2 * RK), :], odd_low[:, j % (2 * RK), :]
            return even_high[:, j // 2 % RK, :], even_low[:, j // 2 % RK, :]

        def nth_split(i, j, t):
            return nth(i, j) if t == 1 else nth_of_kind(i, j)

        def exists(i, j):
            return not isinstance(i, int) or 0 <= nth(i, j) < NG

        def at_least(i, j, n):
            return not isinstance(i, int) or nth(i, j) >= n

        def turns(eng, step, steps):
            for j in range(T):
                step(0, j)
            with eng.Fori(1, TURNS) as i:
                for j in range(T):
                    step(i, j)
            for k in range(TURNS * T, steps):
                step(k // T, k % T)

        def is_block(g):
            return not isinstance(g, int) or g < NB

        def prepare_turns(eng, block_work, batch, ahead=False):
            def turn(o):
                for par in range(2):
                    own = range(FIRST) if par == 0 else range(FIRST, BPT)
                    if ahead:
                        block_work(o * 2 + EARLY + par, par, o)
                    for m in own:
                        batch(o * BPT + m, m % RB)
                        if m == own[-1] and not ahead:
                            block_work(o * 2 + EARLY + par, par, o)

            with eng.Fori(0, PAIRS - 1) as o:
                turn(o)
            turn(PAIRS - 1)

        block = ctx.enter_context(nc.Block())

        @block.sync
        def _(sp):
            sp.dma_start(acc[:, 0:EARLY, :], x[0:EARLY * P, :].rearrange("(b p) d -> p b d", p=P)).then_inc(x_in[0], 16)
            sp.dma_start(src_i[:], src.rearrange("(p c) -> p c", p=EP)).then_inc(src_in, 16)
            sp.dma_start(dst_i[:], dst.rearrange("(p c) -> p c", p=EP)).then_inc(dst_in, 16)
            for part in range(2):
                sp.dma_start(w_sb[:, part * KC:(part + 1) * KC, :],
                             wt[part * D:(part + 1) * D, :].rearrange("(c p) o -> p c o", p=P)).then_inc(w_in[part], 16)
            sp.dma_start(acc[:, EARLY:NB - 1, :],
                         x[EARLY * P:(NB - 1) * P, :].rearrange("(b p) d -> p b d", p=P)).then_inc(x_in[1], 16)
            sp.wait_ge(rest_zero, 1)
            sp.dma_start(acc[0:LAST, NB - 1, :], x[(NB - 1) * P:N, :]).then_inc(x_in[1], 16)
            sp.dma_start(b_sb[:], bias.rearrange("(a d) -> a d", a=1).to_broadcast([P, D])).then_inc(b_in, 16)
            for g in range(NB):
                rows = P if g < NB - 1 else LAST
                sp.wait_ge(v_copied, g + 1)
                sp.dma_start(v_rows[g * P:g * P + rows, :], v_out[0:rows, g % 2, :]).then_inc(v_stored[g % 2], 16)
            sp.wait_ge(groups_ready, 2)
            for g in range(NB - 1):
                end = sp.value_load(end_i[0:1, g:g + 1], min_val=1, max_val=NG)
                sp.wait_ge(added, end)
                sp.dma_start(out[g * P:(g + 1) * P, :], acc[:, g, :]).then_inc(out_stored, 16)
            sp.wait_ge(added, NG)
            sp.dma_start(out[(NB - 1) * P:N, :], acc[0:LAST, NB - 1, :]).then_inc(out_stored, 16)
            sp.wait_ge(out_stored, 16 * NB)

        @block.gpsimd
        def _(pool):
            nc.gpsimd.iota(iota1[:], pattern=[[1, P]], base=1, channel_multiplier=0,
                           allow_small_or_imprecise_dtypes=True).then_inc(first_consts, 1)
            nc.gpsimd.iota(pcol[:], pattern=[[1, 1]], base=1, channel_multiplier=1,
                           allow_small_or_imprecise_dtypes=True).then_inc(first_consts, 1)
            nc.gpsimd.memset(acc[:, NB - 1, :], 0.0).then_inc(rest_zero, 1)
            nc.gpsimd.memset(zeros[:], 0.0).then_inc(consts, 1)
            nc.gpsimd.iota(iota16[:], pattern=[[1, NT]], base=0, channel_multiplier=0,
                           allow_small_or_imprecise_dtypes=True).then_inc(consts, 1)
            nc.gpsimd.iota(iota_b[:], pattern=[[1, P], [0, B]], base=0, channel_multiplier=0,
                           allow_small_or_imprecise_dtypes=True).then_inc(consts, 1)
            nc.gpsimd.iota(group_no[:], pattern=[[1, NG]], base=0, channel_multiplier=0,
                           allow_small_or_imprecise_dtypes=True).then_inc(pool_step, 1)
            pool.wait_ge(dst_in, 16)
            nc.gpsimd.tensor_scalar(over[:], dst_i[:], float(1 << LOW), None, ALU.is_ge)
            nc.gpsimd.tensor_scalar(dst_frac[:], dst_i[:], 2.0 ** -LOW, 1.0, ALU.mult, ALU.add).then_inc(dst_step, 1)
            pool.wait_ge(dst_step, 1)
            nc.gpsimd.tensor_scalar(sign[:], over[:], -2.0, 1.0, ALU.mult, ALU.add)
            nc.gpsimd.tensor_tensor(dst_frac[:], dst_frac[:], over[:], ALU.subtract).then_inc(dst_step, 1)
            pool.wait_ge(dst_step, 2)
            nc.gpsimd.tensor_tensor(dst_frac[:], dst_frac[:], sign[:], ALU.mult).then_inc(dst_ready, 1)
            pool.wait_ge(ends_ready, 1)
            for b in range(NB - 1):
                pool.wait_ge(pool_step, 2 * b + 1)
                nc.gpsimd.tensor_scalar(ended[:], group_no[:], g_end[0:1, b:b + 1], None,
                                        ALU.is_ge).then_inc(pool_step, 1)
                pool.wait_ge(pool_step, 2 * b + 2)
                if b == 0:
                    nc.gpsimd.tensor_copy(gb_f[:], ended[:]).then_inc(pool_step, 1)
                else:
                    nc.gpsimd.tensor_tensor(gb_f[:], gb_f[:], ended[:], ALU.add).then_inc(pool_step, 1)
            pool.wait_ge(pool_step, 2 * NB - 1)
            nc.gpsimd.tensor_copy(gb_i[:], gb_f[:]).then_inc(groups_ready, 1)
            nc.gpsimd.tensor_scalar(end_i[:], g_end[0:1, :], 1.0, None, ALU.max).then_inc(groups_ready, 1)
            for g in range(NB):
                pool.wait_ge(u_high, g + 1)
                nc.gpsimd.tensor_tensor(u2[:, 1, g, :], u_f[:, g % 2, :], u2[:, 0, g, :],
                                        ALU.subtract).then_inc(u_low, 1)
            for par in range(2):
                pool.wait_ge(v_stored[par], 16 * ((NB + 1 - par) // 2))
            pool.wait_ge(window_ready, 1)

            def gather(j, t, **add):
                r = j % RG
                nc.gpsimd.indirect_dma_start(
                    out=v_t[:, r, t, :], out_offset=None, in_=v_rows,
                    in_offset=bass.IndirectOffsetOnAxis(ap=window[:, r * GROUP + t:r * GROUP + t + 1], axis=0),
                    **add).then_inc(v_landed[r][t], 16)

            gather(0, 1)

            def step(i, j):
                pool.wait_ge(u_placed[0], nth(i, j) + 1)
                pool.sem_inc(gathers_let, 1)
                gather(j, 0, compute_op=ALU.add)
                if is_placed(j, 1):
                    pool.wait_ge(u_placed[1], nth_of_kind(i, j) + 1)
                    pool.sem_inc(gathers_let, 1)
                    gather(j, 1, compute_op=ALU.add)
                elif exists(i, j + GATHER_AHEAD):
                    if at_least(i, j + GATHER_AHEAD, RG):
                        pool.wait_ge(pre_ready, nth_of_kind(i, j + GATHER_AHEAD - RG) + 1)
                        pool.sem_inc(gathers_let, 1)
                    gather(j + GATHER_AHEAD, 1)

            turns(pool, step, NG)

        @block.vector
        def _(dve):
            chain = [0]

            def link(ins):
                chain[0] += 1
                ins.then_inc(dve_step, 1)
                dve.wait_ge(dve_step, chain[0])

            def statistics(first, last, part):
                dve.wait_ge(x_in[part], 16 if part == 0 else 32)
                for b in range(first, last):
                    rows = P if b < NB - 1 else LAST
                    ins = nc.vector.bn_stats(stats[0:rows, b, :], acc[0:rows, b, :])
                link(ins)
                for b in range(first, last):
                    rows = P if b < NB - 1 else LAST
                    ins = nc.vector.bn_aggr(mv[0:rows, b, :], stats[0:rows, b, :])
                ins.then_inc(mv_ready, 1)

            def norms(first, last, part):
                dve.wait_ge(std_ready, part + 1)
                link(nc.vector.reciprocal(rstd[:, first:last], std[:, first:last]))
                nc.vector.scalar_tensor_tensor(nmr[:, first:last], mv[:, first:last, 0], -1.0, rstd[:, first:last],
                                               ALU.mult, ALU.mult).then_inc(norm_ready, 1)

            def bias_u(g, par, o):
                dve.wait_ge(u_done, g + 1)
                if o is not None:
                    dve.wait_ge(u_low, g - 1)
                nc.vector.tensor_tensor(u_f[:, par, :], ps_u[par][:], b_sb[:], ALU.add).then_inc(u_biased, 1)

            nc.vector.memset(ones[:], 1.0)
            nc.vector.memset(eps_col[:], EPS)
            nc.vector.memset(mv[:, NB - 1, :], 0.0)
            dve.wait_ge(first_consts, 2)
            nc.vector.tensor_scalar(ident[:], iota1[:], pcol[:], None, ALU.is_equal)
            nc.vector.tensor_scalar(earlier[:], iota1[:], pcol[:], None, ALU.is_gt).then_inc(masks, 1)
            nc.vector.tensor_scalar(ident_r[:], iota1[:], pcol[:], None, ALU.is_equal)
            statistics(0, EARLY, 0)

            dve.wait_ge(src_in, 16)
            nc.vector.tensor_scalar(blk_i[:], src_i[:], 7, None, ALU.arith_shift_right)
            link(nc.vector.tensor_scalar(tmp_i[:], src_i[:], P - 1, FRACTION, ALU.bitwise_and, ALU.logical_shift_left))
            norms(0, EARLY, 0)
            nc.vector.tensor_scalar(node_exp[:], tmp_i[:], float((NODE_EXP + 1) << FRACTION), None, ALU.add)
            link(nc.vector.tensor_copy(blk_f[:], blk_i[:]))
            for b in range(NB):
                last = nc.vector.tensor_scalar(in_blk[:, b, :], blk_f[:], float(b), None, ALU.is_equal)
            link(last)
            for b in range(NB):
                last = nc.vector.tensor_tensor_scan(running[:, b, :], ones[0:EP, 0:EC], in_blk[:, b, :],
                                                    0.0, ALU.mult, ALU.add)
            link(last)
            nc.vector.tensor_copy(cnt[:], running[:, :, EC - 1]).then_inc(counted, 1)

            dve.wait_ge(summed, 1)
            link(nc.vector.tensor_scalar(tot_i[:], ps_cnt[:, 16:16 + NB], float(GS - 1), None, ALU.add))
            link(nc.vector.tensor_scalar(ngr_i[:], tot_i[:], GS.bit_length() - 1, None, ALU.arith_shift_right))
            link(nc.vector.tensor_copy(ngr[:], ngr_i[:]))
            link(nc.vector.tensor_tensor_scan(g_end[:], ones[:, 0:NB], ngr[:], 0.0, ALU.mult, ALU.add))
            dve.sem_inc(ends_ready, 1)
            link(nc.vector.tensor_tensor(g_start[:], g_end[:], ngr[:], ALU.subtract))
            link(nc.vector.tensor_scalar(off[:], g_start[:], float(GS), -1.0, ALU.mult, ALU.add))
            link(nc.vector.tensor_tensor(off[0:EP, :], off[0:EP, :], ps_cnt[0:EP, 0:NB], ALU.add))
            statistics(EARLY, NB, 1)
            for b in range(NB):
                last = nc.vector.scalar_tensor_tensor(running[:, b, :], running[:, b, :], off[0:EP, b:b + 1],
                                                      in_blk[:, b, :], ALU.add, ALU.mult)
                if b == 0:
                    norms(EARLY, NB, 1)
                    dve.wait_ge(b_in, 16)
                    bias_u(0, 0, None)
            link(last)
            bias_u(1, 1, None)
            link(nc.vector.tensor_reduce(pos[:], running[:].rearrange("p b c -> p c b"),
                                         mybir.AxisListType.X, ALU.add))
            link(nc.vector.tensor_copy(pos_i[:], pos[:]))
            nc.vector.tensor_scalar(blk_i[:], pos_i[:], 7, None, ALU.arith_shift_right)
            link(nc.vector.tensor_scalar(tmp_i[:], pos_i[:], P - 1, None, ALU.bitwise_and))
            nc.vector.tensor_copy(pos_lo[:], tmp_i[:])
            link(nc.vector.tensor_copy(pos_hi[:], blk_i[:]))
            dve.wait_ge(consts, 3)

            def batch(m, par):
                dve.wait_ge(room, m + 1)
                cols = bass.ds(m * B, B)
                def over_slots(t):
                    return t[:, cols].rearrange("p (a c) -> p a c", a=1).to_broadcast([EP, P, B])
                nc.vector.tensor_tensor(hot_lo[:, par], iota_b[0:EP], over_slots(pos_lo),
                                        ALU.is_equal).then_inc(lo_ready, 1)
                for c in range(B):
                    col = bass.ds(m * B + c, 1)
                    last = nc.vector.tensor_scalar(hot_hi[:, par, c, :], iota16[0:EP, :], pos_hi[:, col],
                                                   node_exp[:, col].bitcast(F32), ALU.is_equal, ALU.mult)
                last.then_inc(operands_hi, 1)

            prepare_turns(dve, bias_u, batch)

            def decode(first, last):
                bits = place[:, first:last].bitcast(I32)
                for field, shift, mask in ((node_bits, FRACTION, 2 * BIAS + 1), (low_bits, FRACTION - LOW, (1 << LOW) - 1),
                                           (high_bits, 31 - LOW, 1 << LOW)):
                    ins = nc.vector.tensor_scalar(field[:, first:last], bits, shift, mask,
                                                  ALU.arith_shift_right, ALU.bitwise_and)
                link(ins)
                nc.vector.tensor_tensor(slot_dst[:, first:last], low_bits[:, first:last], high_bits[:, first:last],
                                        ALU.add).then_inc(heads_ready, 1)
                nc.vector.tensor_scalar(slot_node1[:, first:last], node_bits[:, first:last], -float(NODE_EXP), 0.0,
                                        ALU.add, ALU.max).then_inc(tables_ready, 1)

            dve.wait_ge(room, BATCHES + RB)
            decode(0, RG * GROUP)
            dve.wait_ge(tables_ready, 1)

            def one_hots(i, j):
                if at_least(i, j, RG):
                    dve.wait_ge(summed_groups, nth(i, j - RG) + 1)
                of_slot = slot_node1[:, bass.ds(nth(i, j) * GROUP, GROUP)].rearrange("p (t a) -> p t a", a=1)
                nodes = iota1[:].rearrange("p (a n) -> p a n", a=1)
                nc.vector.tensor_tensor(hot[:, j % RG], nodes.to_broadcast([P, GROUP, P]),
                                        of_slot.to_broadcast([P, GROUP, P]), ALU.is_equal).then_inc(hot_ready, 1)

            for j in range(HOT_AHEAD):
                one_hots(0, j)
            decode(RG * GROUP, NT)
            dve.wait_ge(tables_ready, 2)

            def step(i, j):
                g = j - ADD_LAG
                if at_least(i, g, 0):
                    b = dve.value_load(gb_i[0:1, bass.ds(nth(i, g), 1)], min_val=0, max_val=NB - 1)
                    dve.wait_ge(summed_groups, nth(i, g) + 1)
                    if at_least(i, g, 1):
                        dve.wait_ge(added, nth(i, g))
                    a = acc[:, bass.ds(b, 1), :].rearrange("p a d -> p (a d)")
                    nc.vector.tensor_tensor(a, a, ps_agg[g % 2][:], ALU.add).then_inc(added, 1)
                if exists(i, j + HOT_AHEAD):
                    one_hots(i, j + HOT_AHEAD)
                g = j - SPLIT_LAG
                for t in (1, 0):
                    if is_split(g, t) and exists(i, g):
                        high, low = parts_of(g, t)
                        dve.wait_ge(msg_ready[t], nth(i, g) + 1)
                        nc.vector.scalar_tensor_tensor(low, rows_of(g, t), 0.0, high, ALU.max,
                                                       ALU.subtract).then_inc(split_ready[t], 1)
                if not is_placed(j, 1) and exists(i, j):
                    dve.wait_ge(v_landed[j % RG][1], 16 * nth_in_place(i, j))
                    dve.wait_ge(spread[1], nth(i, j) + 1)
                    nc.vector.tensor_tensor(pre[:, j // 2 % RA, :], v_t[:, j % RG, 1, :],
                                            ps_spread[j % 2 * GROUP + 1][:], ALU.add).then_inc(pre_ready, 1)

            turns(dve, step, NG + ADD_LAG)

        @block.scalar
        def _(act):
            def normalize(g, par):
                nc.scalar.activation(h[:, par, :], acc[:, bass.ds(g, 1), :].rearrange("p a d -> p (a d)"),
                                     ACT.Relu, bias=nmr[:, bass.ds(g, 1)],
                                     scale=rstd[:, bass.ds(g, 1)]).then_inc(h_ready, 1)

            def turned_h(g, par):
                act.wait_ge(hT_done, g + 1)
                nc.scalar.copy(hT[:, par, :], ps_hT[:]).then_inc(hT_ready, 1)

            def parts(g, par, o):
                act.wait_ge(v_done, g + 1)
                if o is not None:
                    act.wait_ge(v_stored[par], 16 * (o + 1))
                nc.scalar.copy(v_out[:, par, :], ps_v[par][:]).then_inc(v_copied, 1)
                act.wait_ge(u_biased, g + 1)
                nc.scalar.copy(u2[:, 0, bass.ds(g, 1), :].rearrange("p a d -> p (a d)"),
                               u_f[:, par, :]).then_inc(u_high, 1)

            act.wait_ge(mv_ready, 1)
            nc.scalar.activation(std[:, 0:EARLY], mv[:, 0:EARLY, 1], ACT.Sqrt, bias=eps_col[:]).then_inc(std_ready, 1)
            act.wait_ge(norm_ready, 1)
            for g in range(EARLY):
                normalize(g, g)
            turned_h(0, 0)
            turned_h(1, 1)
            act.wait_ge(mv_ready, 2)
            nc.scalar.activation(std[:, EARLY:NB], mv[:, EARLY:NB, 1], ACT.Sqrt,
                                 bias=eps_col[:]).then_inc(std_ready, 1)
            act.wait_ge(norm_ready, 2)
            normalize(2, 0)
            normalize(3, 1)
            act.wait_ge(v_done, 1)
            turned_h(2, 0)
            parts(0, 0, None)
            parts(1, 1, None)

            def block_work(g, par, o):
                parts(g, par, o)
                if is_block(g + 1):
                    turned_h(g + 1, 1 - par)
                if is_block(g + 2):
                    normalize(g + 2, par)

            def batch(m, par):
                act.wait_ge(lo_ready, m + 1)
                for c in range(B):
                    ins = nc.scalar.activation(hot_lo_d[:, par, c, :], hot_lo[:, par, :, c], ACT.Copy,
                                               scale=dst_frac[:, bass.ds(m * B + c, 1)])
                ins.then_inc(operands_lo, 1)

            act.wait_ge(dst_ready, 1)
            prepare_turns(act, block_work, batch)

            act.wait_ge(heads_ready, 1)
            nc.scalar.copy(window[:], slot_dst[:, 0:RG * GROUP]).then_inc(window_ready, 1)

            def turned(i, j):
                act.wait_ge(hotT_done, nth(i, j) + 1)
                nc.scalar.copy(hotT[:, j % 2].rearrange("p t n -> p (t n)"),
                               ps_hotT[j % 2][:, 0:GROUP * P]).then_inc(hotT_ready, 1)

            turned(0, 0)
            act.wait_ge(heads_ready, 2)

            def step(i, j):
                if exists(i, j + 1):
                    turned(i, j + 1)
                for t in range(GROUP):
                    if is_placed(j, t) and exists(i, j):
                        act.wait_ge(spread[t], nth(i, j) + 1)
                        nc.scalar.copy(v_t[:, j % RG, t, :], ps_spread[j % 2 * GROUP + t][:]).then_inc(u_placed[t], 1)
                g = j - RELU_LAG
                if exists(i, g):
                    if not exists(i, j + 1):
                        act.wait_ge(summed_groups, nth(i, g - 2 * RK) + 1)
                    for t in (1, 0):
                        if is_placed(g, t):
                            act.wait_ge(v_landed[g % RG][t], 16 * nth_in_place(i, g))
                        else:
                            act.wait_ge(pre_ready, nth_of_kind(i, g) + 1)
                        message = parts_of(g, t)[0] if is_split(g, t) else msg[:, g // 2 % RA, :]
                        nc.scalar.activation(message, rows_of(g, t), ACT.Relu).then_inc(msg_ready[t], 1)
                    if g % WG == WG - 1 and exists(i, g + RG):
                        w = (g - WG + 1) % RG * GROUP
                        nc.scalar.copy(window[:, w:w + WG * GROUP],
                                       slot_dst[:, bass.ds(nth(i, g - WG + 1 + RG) * GROUP, WG * GROUP)])

            turns(act, step, NG + RELU_LAG)

        @block.tensor
        def _(pe):
            def turn_h(g, par):
                pe.wait_ge(h_ready, g + 1)
                for c in range(KC):
                    last = nc.tensor.transpose(ps_hT[:, c * P:(c + 1) * P], h[:, par, c * P:(c + 1) * P], ident[:])
                last.then_inc(hT_done, 1)

            def product(g, par, o, between=None):
                pe.wait_ge(hT_ready, g + 1)
                if o is not None:
                    pe.wait_ge(u_biased, g - 1)
                else:
                    pe.wait_ge(w_in[0], 16)
                for c in range(KC):
                    if c == KC - 2 and between is not None:
                        between()
                    last = nc.tensor.matmul(ps_u[par][:], hT[:, par, c * P:(c + 1) * P], w_sb[:, c, :],
                                            start=(c == 0), stop=(c == KC - 1))
                last.then_inc(u_done, 1)
                if o is not None:
                    pe.wait_ge(v_copied, g - 1)
                else:
                    pe.wait_ge(w_in[1], 16)
                for c in range(KC):
                    last = nc.tensor.matmul(ps_v[par][:], hT[:, par, c * P:(c + 1) * P], w_sb[:, KC + c, :],
                                            start=(c == 0), stop=(c == KC - 1))
                last.then_inc(v_done, 1)

            pe.sem_inc(room, RB)
            pe.wait_ge(masks, 1)
            turn_h(0, 0)
            pe.wait_ge(hT_ready, 1)
            turn_h(1, 1)

            def sum_counts():
                pe.wait_ge(counted, 1)
                nc.tensor.matmul(ps_cnt[0:EP, 0:NB], earlier[0:EP, 0:EP], cnt[:], start=True, stop=True)
                nc.tensor.matmul(ps_cnt[:, 16:16 + NB], ones[0:EP, 0:P], cnt[:], start=True, stop=True).then_inc(summed, 1)

            product(0, 0, None, between=sum_counts)
            product(1, 1, None)
            turn_h(2, 0)

            pe.wait_ge(consts, 2)
            nc.tensor.matmul(place[:, 0:NT], zeros[:], iota16[0:EP, :], start=True, stop=False,
                             skip_group_check=True)

            def block_work(g, par, o):
                product(g, par, o)
                if is_block(g + 1):
                    turn_h(g + 1, 1 - par)

            def batch(m, par):
                pe.wait_ge(operands_lo, m + 1)
                pe.wait_ge(operands_hi, m + 1)
                for c in range(B):
                    end = isinstance(m, int) and m == BATCHES - 1 and c == B - 1
                    last = nc.tensor.matmul(place[:, 0:NT], hot_lo_d[:, par, c, :], hot_hi[:, par, c, :],
                                            start=False, stop=end, skip_group_check=True)
                last.then_inc(room, 1)

            prepare_turns(pe, block_work, batch, ahead=True)

            pe.wait_ge(groups_ready, 2)
            pe.wait_ge(u_low, NB)

            def turn_hots(i, j):
                pe.wait_ge(hot_ready, nth(i, j) + 1)
                for t in range(GROUP):
                    last = nc.tensor.matmul(ps_hotT[j % 2][:, t * P:(t + 1) * P], hot[:, j % RG, t, :], ident_r[:],
                                            start=True, stop=True)
                last.then_inc(hotT_done, 1)

            turn_hots(0, 0)

            def step(i, j):
                if exists(i, j):
                    b = pe.value_load(gb_i[0:1, bass.ds(nth(i, j), 1)], min_val=0, max_val=NB - 1)
                if exists(i, j + 1):
                    turn_hots(i, j + 1)
                if exists(i, j):
                    pe.wait_ge(hotT_ready, nth(i, j) + 1)
                    if not is_placed(j, 1) and at_least(i, j, 2):
                        pe.wait_ge(pre_ready, nth_of_kind(i, j))
                    for t in range(GROUP):
                        for part in range(2):
                            last = nc.tensor.matmul(
                                ps_spread[j % 2 * GROUP + t][:], hotT[:, j % 2, t, :],
                                u2[:, part, bass.ds(b, 1), :].rearrange("p a d -> p (a d)"),
                                start=(part == 0), stop=(part == 1))
                        last.then_inc(spread[t], 1)
                g = j - SUM_LAG
                if at_least(i, g, 0):
                    if at_least(i, g, 2):
                        pe.wait_ge(added, nth(i, g) - 1)
                    for t in (1, 0):
                        nodes = hot[:, g % RG, t, :]
                        if is_split(g, t):
                            pe.wait_ge(split_ready[t], nth_split(i, g, t) + 1)
                            products = [(nodes, part) for part in parts_of(g, t)]
                        else:
                            pe.wait_ge(msg_ready[t], nth(i, g) + 1)
                            products = [(nodes.bitcast(F32), msg[:, g // 2 % RA, :])]
                        for n, (lhsT, rhs) in enumerate(products):
                            last = nc.tensor.matmul(ps_agg[g % 2][:], lhsT, rhs, start=(t == 1 and n == 0),
                                                    stop=(t == 0 and n == len(products) - 1))
                    last.then_inc(summed_groups, 1)

            turns(pe, step, NG + SUM_LAG)


def kernel(**inputs):
    import numpy as np
    import concourse.bacc as bacc
    from concourse.bass_utils import run_bass_kernel_spmd

    nc = bacc.Bacc("TRN2", target_bir_lowering=False, num_devices=1)
    laid = {
        "x": np.ascontiguousarray(inputs["x"]),
        "src": np.ascontiguousarray(inputs["src"]),
        "dst": np.ascontiguousarray(inputs["dst"]),
        "wt": np.ascontiguousarray(np.asarray(inputs["L0_gnn_W"]).T),
        "bias": np.ascontiguousarray(inputs["L0_gnn_b"]),
    }
    args = {k: nc.dram_tensor(f"in_{k}", a.shape, mybir.dt.from_np(a.dtype), kind="ExternalInput").ap()
            for k, a in laid.items()}
    out = nc.dram_tensor("out_0", laid["x"].shape, F32, kind="ExternalOutput").ap()
    bass_gnn_edge_messages(nc, args["x"], args["src"], args["dst"], args["wt"], args["bias"], out)
    r = run_bass_kernel_spmd(nc, [{f"in_{k}": a for k, a in laid.items()}], core_ids=[0])
    return r.results[0]["out_0"]
```
